# Optimizing a Trainium2 kernel written in Bass

```python
import numpy as np
import jax
import jax.numpy as jnp

def _softmax(x, axis=-1):
    return jax.nn.softmax(x, axis=axis)

def _gelu(x):
    return jax.nn.gelu(x, approximate=True)

def _silu(x):
    return jax.nn.silu(x)

def _sigmoid(x):
    return jax.nn.sigmoid(x)

def _layernorm(x, axis=-1, eps=1e-05):
    m = jnp.mean(x, axis=axis, keepdims=True)
    v = jnp.var(x, axis=axis, keepdims=True)
    return (x - m) / jnp.sqrt(v + eps)

def _scatter_add(tgt, idx, src, axis=0):
    return tgt.at[idx].add(src)

def _segment_sum(src, seg, n):
    return jax.ops.segment_sum(src, seg, n)
kernel_name = 'mk_gnn_resnorm_d2_gnn_r16_2f83c0'

def setup_inputs(seed: int=0):
    np.random.seed(seed)
    _w = jnp.asarray

    def _rec_inputs():
        import jax
        import jax.numpy as jnp
        _gk = jax.random.key(seed)
        x = -8.776e-05 + 1 * jax.random.normal(jax.random.fold_in(_gk, 1), (2500, 128), jnp.float32)
        _s = jax.random.randint(jax.random.fold_in(_gk, 2), (40000,), 0, 2500, jnp.int32)
        _d = jax.random.randint(jax.random.fold_in(_gk, 3), (40000,), 0, 2500, jnp.int32)
        _loop = jnp.arange(2500, dtype=jnp.int32)
        src = jnp.concatenate([_s, _d, _loop])
        dst = jnp.concatenate([_d, _s, _loop])
        _o = jnp.argsort(dst, stable=True)
        src = src[_o]
        dst = dst[_o]
        edge_attr_100 = 0.000154925 + 1.00009 * jax.random.normal(jax.random.fold_in(_gk, 12), (82500, 100), jnp.float32)
        edge_weight = jax.random.uniform(jax.random.fold_in(_gk, 14), (82500,), jnp.float32, 0.0, 0.999998)
        return (x, src, dst, edge_attr_100, edge_weight)
    x, src, dst, edge_attr_100, edge_weight = _rec_inputs()

    def _L0_gnn_setup():
        import jax, jax.numpy as jnp
        import numpy as np
        N = 2500
        E = 25000
        H = 128
        F = 128
        G = 100
        L = 6
        CUTOFF = 10.0
        PI = float(np.pi)
        LOG2 = float(np.log(2.0))

        def ssp(x):
            return jax.nn.softplus(x) - LOG2
        key = jax.random.key(seed)
        ks = jax.random.split(key, 14)
        s = 0.05
        return {'z': jax.random.normal(ks[0], (N, H), dtype=jnp.float32), 'edge_index': jax.random.randint(ks[1], (2, E), 0, N), 'edge_length': jax.random.uniform(ks[2], (E,), dtype=jnp.float32), 'edge_attr': jax.random.normal(ks[3], (E, G), dtype=jnp.float32), 'mlp_w1': jax.random.normal(ks[4], (L, G, F), dtype=jnp.float32) * s, 'mlp_b1': jnp.zeros((L, F), dtype=jnp.float32), 'mlp_w2': jax.random.normal(ks[5], (L, F, F), dtype=jnp.float32) * s, 'mlp_b2': jnp.zeros((L, F), dtype=jnp.float32), 'conv_w1': jax.random.normal(ks[6], (L, H, F), dtype=jnp.float32) * s, 'conv_w2': jax.random.normal(ks[7], (L, F, H), dtype=jnp.float32) * s, 'conv_b2': jnp.zeros((L, H), dtype=jnp.float32), 'lin_w': jax.random.normal(ks[8], (L, H, H), dtype=jnp.float32) * s, 'lin_b': jnp.zeros((L, H), dtype=jnp.float32)}
    _L0_gnn_all = _L0_gnn_setup()
    _L0_gnn_in = {k: v for k, v in _L0_gnn_all.items() if k in ('mlp_w1', 'mlp_b1', 'mlp_w2', 'mlp_b2', 'conv_w1', 'conv_w2', 'conv_b2', 'lin_w', 'lin_b')}
    del _L0_gnn_all

    def _L1_gnn_setup():
        import jax, jax.numpy as jnp
        import numpy as np
        N_NODES = 3125
        N_EDGES = 50000
        D = 128
        L = 3
        key = jax.random.key(seed)
        ks = jax.random.split(key, 8)
        h = jax.random.normal(ks[0], (N_NODES, D), dtype=jnp.float32)
        src = jax.random.randint(ks[1], (N_EDGES,), 0, N_NODES, dtype=jnp.int32)
        dst = jax.random.randint(ks[2], (N_EDGES,), 0, N_NODES, dtype=jnp.int32)
        w_scale = 0.05
        W1 = jax.random.normal(ks[3], (L, D, D), dtype=jnp.float32) * w_scale
        b1 = jnp.zeros((L, D), dtype=jnp.float32)
        W2 = jax.random.normal(ks[4], (L, D, D), dtype=jnp.float32) * w_scale
        b2 = jnp.zeros((L, D), dtype=jnp.float32)
        eps = jnp.zeros((L,), dtype=jnp.float32)
        return {'h': h, 'src': src, 'dst': dst, 'W1': W1, 'b1': b1, 'W2': W2, 'b2': b2, 'eps': eps}
    _L1_gnn_all = _L1_gnn_setup()
    _L1_gnn_in = {k: v for k, v in _L1_gnn_all.items() if k in ('W1', 'b1', 'W2', 'b2', 'eps')}
    del _L1_gnn_all
    return {'x': x, 'src': src, 'dst': dst, 'edge_attr_100': edge_attr_100, 'edge_weight': edge_weight, 'L0_gnn_mlp_w1': _L0_gnn_in['mlp_w1'], 'L0_gnn_mlp_b1': _L0_gnn_in['mlp_b1'], 'L0_gnn_mlp_w2': _L0_gnn_in['mlp_w2'], 'L0_gnn_mlp_b2': _L0_gnn_in['mlp_b2'], 'L0_gnn_conv_w1': _L0_gnn_in['conv_w1'], 'L0_gnn_conv_w2': _L0_gnn_in['conv_w2'], 'L0_gnn_conv_b2': _L0_gnn_in['conv_b2'], 'L0_gnn_lin_w': _L0_gnn_in['lin_w'], 'L0_gnn_lin_b': _L0_gnn_in['lin_b'], 'L1_gnn_W1': _L1_gnn_in['W1'], 'L1_gnn_b1': _L1_gnn_in['b1'], 'L1_gnn_W2': _L1_gnn_in['W2'], 'L1_gnn_b2': _L1_gnn_in['b2'], 'L1_gnn_eps': _L1_gnn_in['eps']}

def reference(x, src, dst, edge_attr_100, edge_weight, L0_gnn_mlp_w1, L0_gnn_mlp_b1, L0_gnn_mlp_w2, L0_gnn_mlp_b2, L0_gnn_conv_w1, L0_gnn_conv_w2, L0_gnn_conv_b2, L0_gnn_lin_w, L0_gnn_lin_b, L1_gnn_W1, L1_gnn_b1, L1_gnn_W2, L1_gnn_b2, L1_gnn_eps):
    import jax
    import jax.numpy as jnp

    def _L0_gnn_ref(z, edge_index, edge_length, edge_attr, mlp_w1, mlp_b1, mlp_w2, mlp_b2, conv_w1, conv_w2, conv_b2, lin_w, lin_b):
        import jax, jax.numpy as jnp
        import numpy as np
        N = 2500
        E = 25000
        H = 128
        F = 128
        G = 100
        L = 6
        CUTOFF = 10.0
        PI = float(np.pi)
        LOG2 = float(np.log(2.0))

        def ssp(x):
            return jax.nn.softplus(x) - LOG2
        src = edge_index[0]
        dst = edge_index[1]
        C = 0.5 * (jnp.cos(edge_length * PI / CUTOFF) + 1.0)
        C = C * (edge_length <= CUTOFF) * (edge_length >= 0.0)
        h = z
        for l in range(L):
            W = ssp(edge_attr @ mlp_w1[l] + mlp_b1[l]) @ mlp_w2[l] + mlp_b2[l]
            W = W * C[:, None]
            xf = h @ conv_w1[l]
            msg = xf[src] * W
            agg = jax.ops.segment_sum(msg, dst, num_segments=N)
            x2 = agg @ conv_w2[l] + conv_b2[l]
            h = h + (ssp(x2) @ lin_w[l] + lin_b[l])
        return h

    def _L1_gnn_ref(h, src, dst, W1, b1, W2, b2, eps):
        import jax, jax.numpy as jnp
        import numpy as np
        N_NODES = 3125
        N_EDGES = 50000
        D = 128
        L = 3
        n = h.shape[0]
        for l in range(W1.shape[0]):
            agg = jax.ops.segment_sum(h[src], dst, num_segments=n)
            z = (1.0 + eps[l]) * h + agg
            hid = jnp.maximum(z @ W1[l] + b1[l], 0.0)
            h = hid @ W2[l] + b2[l]
        return h
    edge_index = jnp.stack([src, dst])
    x = _layernorm(x + _L0_gnn_ref(x, edge_index, edge_weight, edge_attr_100, L0_gnn_mlp_w1, L0_gnn_mlp_b1, L0_gnn_mlp_w2, L0_gnn_mlp_b2, L0_gnn_conv_w1, L0_gnn_conv_w2, L0_gnn_conv_b2, L0_gnn_lin_w, L0_gnn_lin_b), axis=-1)
    x = _layernorm(x + _L1_gnn_ref(x, src, dst, L1_gnn_W1, L1_gnn_b1, L1_gnn_W2, L1_gnn_b2, L1_gnn_eps), axis=-1)
    return x

_drawn_inputs = setup_inputs


def setup_inputs(seed=0):
    import zlib

    import numpy as np

    out = dict(_drawn_inputs(seed))
    spreads = {'L0_gnn_mlp_b1': (0.0, 0.1),
     'L0_gnn_mlp_b2': (0.0, 0.1),
     'L0_gnn_conv_b2': (0.0, 0.1),
     'L0_gnn_lin_b': (0.0, 0.1),
     'L1_gnn_b1': (0.0, 0.1),
     'L1_gnn_b2': (0.0, 0.1),
     'L1_gnn_eps': (0.0, 0.1)}
    factors = {}
    for name, (base, spread) in spreads.items():
        noise = np.random.default_rng([zlib.crc32(name.encode()), seed]).standard_normal(out[name].shape)
        drawn = base * np.exp(spread * noise) if base else spread * noise
        out[name] = jnp.asarray(drawn.astype(out[name].dtype))
    for name, factor in factors.items():
        out[name] = (out[name] * factor).astype(out[name].dtype)
    return out
```

```python
import concourse.bass as bass
from concourse import mybir
from contextlib import ExitStack
import math

P = 128
N = 2500
E = 82500
F = 128
G = 100
L0 = 6
L1 = 3
TPG = 4
GE = TPG * P
U = 6
NG = -(-E // GE)
NIT = NG // U
assert NG % U == 0
EP = NG * GE
WIN = 32
KMAX = N // WIN + 1
CH = 512
NCH = -(-N // CH)
NP = NCH * CH
AGW = N + (KMAX + 1) * WIN
CUTOFF = 10.0
LN2 = math.log(2.0)
XCLAMP = 40.0
LN_EPS = 1e-5

EW_W1, EW_W2, EW_CW1, EW_B1, EW_N = 0, F, 2 * F, 3 * F, 3 * F + 1
NW_CW2, NW_LIN, NW_CB2, NW_LB, NW_N = 0, F, 2 * F, 2 * F + 1, 2 * F + 2
GW_W1, GW_W2, GW_B1, GW_B2, GW_EPS, GW_N = 0, F, 2 * F, 2 * F + 1, 2 * F + 2, 2 * F + 3


def gnn_program(nc, xT_d, src_d, dst_d, ew_d, attr_d, edge_w_d, b2_d, node_w_d, gin_w_d, ident_d, iota_d, out_d):
    f32, i32 = mybir.dt.float32, mybir.dt.int32
    ACT, ALU, AX = mybir.ActivationFunctionType, mybir.AluOpType, mybir.AxisListType
    RMAX = bass.bass_isa.ReduceOp.max
    table_d = nc.dram_tensor("node_table", [NP, F], f32, kind="Internal").ap()

    with ExitStack() as ctx:
        def sb(name, shape, dt=f32):
            return ctx.enter_context(nc.sbuf_tensor(name, shape, dt))

        def psum(name):
            return [ctx.enter_context(nc.psum_tensor(f"{name}{i}", [P, 512], f32)) for i in range(2)]

        def sem(name):
            return ctx.enter_context(nc.semaphore(name))

        def slot_sems(name, n=U):
            return [sem(f"{name}{i}") for i in range(n)]

        xT = sb("xT", [P, NP])
        hT = sb("hT", [P, NP])
        aggT = sb("aggT", [P, AGW])
        stage = sb("stage", [P, NCH, CH])
        ident = sb("ident", [P, P])
        mean_mat = sb("mean_mat", [P, P])
        ones_row = sb("ones_row", [1, P])
        iota = sb("iota", [P, KMAX * WIN])
        half = sb("half", [P, 1])
        half_pi = sb("half_pi", [P, 1])
        eps_col = sb("eps_col", [P, 1])

        edge_w = sb("edge_w", [P, EW_N])
        b1_ln2 = sb("b1_ln2", [P, 1])
        b2_row = sb("b2_row", [1, GE])
        node_w = sb("node_w", [P, NW_N])
        cb2_ln2 = sb("cb2_ln2", [P, 1])
        gin_w = sb("gin_w", [P, GW_N])
        eps1 = sb("eps1", [P, 1])
        dst_i = sb("dst_i", [P, NG * TPG], i32)
        rel = sb("rel", [P, NG * TPG])
        cut = sb("cut", [P, NG * TPG])
        len_raw = sb("len_raw", [P, NG * TPG])
        len_mask = sb("len_mask", [P, NG * TPG])
        ends = sb("ends", [P, 2, NG])
        ends_all = sb("ends_all", [P, 2, NG])
        base_f = sb("base_f", [P, NG])
        base_i = sb("base_i", [P, NG], i32)
        span = sb("span", [P, NG])
        span_max = sb("span_max", [P, 1])
        span_i = sb("span_i", [P, 1], i32)
        span_s = sb("span_s", [P, 1], i32)
        passes = sb("passes", [P, 1], i32)
        attr = sb("attr", [G, U, GE])
        idx = sb("idx", [P, U, TPG], i32)
        rows = sb("rows", [P, U, GE])
        rel_now = sb("rel_now", [P, U * TPG])
        cut_now = sb("cut_now", [P, U * TPG])
        win_now = sb("win_now", [P, WIN])
        xc = sb("xc", [P, 2, GE])
        ex = sb("ex", [P, 2, GE])
        lg = sb("lg", [P, 2, GE])
        hid = sb("hid", [P, 2, GE])
        msg = sb("msg", [P, 2, GE])
        onehot = sb("onehot", [P, 2, TPG, WIN])

        ps_h, ps_w, ps_a, ps_t = psum("ps_h"), psum("ps_w"), psum("ps_a"), psum("ps_t")

        consts_in, consts_set = sem("consts_in"), sem("consts_set")
        pre = sem("pre")
        ends_reduced, cosine_done, ready = sem("ends_reduced"), sem("cosine_done"), sem("ready")
        edge_w_in, node_w_in, gin_w_in = sem("edge_w_in"), sem("node_w_in"), sem("gin_w_in")
        edge_w_free, node_w_free, gin_w_free = sem("edge_w_free"), sem("node_w_free"), sem("gin_w_free")
        b1_set, cb2_set, eps1_set = sem("b1_set"), sem("cb2_set"), sem("eps1_set")
        table_in = slot_sems("table_in", NCH)
        attr_in, idx_in, rows_in = slot_sems("attr_in"), slot_sems("idx_in"), slot_sems("rows_in")
        mm1_done, clamp_done, log_done, ssp_done = (slot_sems(s) for s in ("mm1_", "clamp_", "log_", "ssp_"))
        mm2_done, msg_done, hot_done, agg_done, add_done = (slot_sems(s) for s in
                                                            ("mm2_", "msg_", "hot_", "agg_", "add_"))
        exp_done = sem("exp_done")
        slices_set, win_set = sem("slices_set"), sem("win_set")
        proj_done, proj_copied = sem("proj_done"), sem("proj_copied")
        n_prod1, n_clamp, n_exp, n_act, n_ssp, n_prod2 = (sem(s) for s in
            ("n_prod1", "n_clamp", "n_exp", "n_act", "n_ssp", "n_prod2"))
        h_done, agg_clear, z_done = sem("h_done"), sem("agg_clear"), sem("z_done")
        ln_sum, ln_mean, ln_dev, ln_sq, ln_var, ln_std, ln_inv, ln_done, ln_keep = (sem(s) for s in
            ("ln_sum", "ln_mean", "ln_dev", "ln_sq", "ln_var", "ln_std", "ln_inv", "ln_done", "ln_keep"))
        out_done = sem("out_done")
        gate = sem("gate")

        table_rows = table_d.rearrange("(c j p) f -> c p j f", j=CH // P, p=P)

        def load_passes(eng):
            eng.wait_ge(ready, 1)
            return eng.value_load(passes[0:1, 0:1], min_val=1, max_val=KMAX)

        def col(t, c):
            return t[:, c * CH:(c + 1) * CH]

        block = ctx.enter_context(nc.Block())

        @block.sync
        def _(sp):
            for t, s in ((dst_i, dst_d), (len_raw, ew_d), (xT, xT_d), (hT, xT_d), (ident, ident_d), (iota, iota_d)):
                sp.dma_start(t[:, :], s).then_inc(consts_in, 16)
            K = load_passes(sp)

            def edge_loads(layer, with_attr):
                with sp.Fori(0, K) as k:
                    with sp.Fori(0, NIT) as it:
                        last = sp.snap(layer * (K * NIT) + k * NIT + it + 1)
                        for u in range(U):
                            g = it * U + u
                            sp.wait_ge(msg_done[u], last)
                            sp.dma_start(idx[:, u, :], src_d[bass.ds(g, 1)].rearrange("a p t -> (a p) t")
                                         ).then_inc(idx_in[u], 16)
                            if with_attr:
                                sp.wait_ge(mm1_done[u], last)
                                sp.dma_start(attr[:, u, :], attr_d[bass.ds(g, 1)].rearrange("a p t -> (a p) t")
                                             ).then_inc(attr_in[u], 16)

            with sp.Fori(0, L0) as layer:
                sp.wait_ge(edge_w_free, layer + 1)
                sp.dma_start(edge_w[:, :], edge_w_d[bass.ds(layer, 1)].rearrange("a p t -> (a p) t")
                             ).then_inc(edge_w_in, 16)
                sp.dma_start(b2_row[:, :], b2_d[bass.ds(layer, 1)].rearrange("a p t -> (a p) t")
                             ).then_inc(edge_w_in, 16)
                sp.wait_ge(node_w_free, layer + 1)
                sp.dma_start(node_w[:, :], node_w_d[bass.ds(layer, 1)].rearrange("a p t -> (a p) t")
                             ).then_inc(node_w_in, 16)
                edge_loads(layer, True)
            with sp.Fori(0, L1) as g:
                sp.wait_ge(gin_w_free, g + 1)
                sp.dma_start(gin_w[:, :], gin_w_d[bass.ds(g, 1)].rearrange("a p t -> (a p) t")
                             ).then_inc(gin_w_in, 16)
                edge_loads(L0 + g, False)

        @block.gpsimd
        def _(pool):
            pool.memset(mean_mat[:, :], 1.0 / F).then_inc(consts_set, 1)
            pool.memset(ones_row[:, :], 1.0).then_inc(consts_set, 1)
            pool.memset(half[:, :], 0.5).then_inc(consts_set, 1)
            pool.memset(half_pi[:, :], math.pi / 2).then_inc(consts_set, 1)
            pool.memset(eps_col[:, :], LN_EPS).then_inc(consts_set, 1)
            pool.wait_ge(pre, 3)
            pool.partition_all_reduce(ends_all[:, :, :].rearrange("p a g -> p (a g)"),
                                      ends[:, :, :].rearrange("p a g -> p (a g)"), P, RMAX).then_inc(ends_reduced, 1)
            K = load_passes(pool)
            with pool.Fori(0, L0 + L1) as layer:
                for c in range(NCH):
                    pool.wait_ge(table_in[c], layer * 16 + 16)
                    pool.sem_inc(gate, 1)
                with pool.Fori(0, K) as k:
                    with pool.Fori(0, NIT) as it:
                        last = pool.snap(layer * (K * NIT) + k * NIT + it + 1)
                        landed = pool.snap(last * 16)
                        for u in range(U):
                            pool.wait_ge(idx_in[u], landed)
                            pool.wait_ge(msg_done[u], last)
                            pool.sem_inc(gate, 1)
                            for t in range(TPG):
                                pool.indirect_dma_start(
                                    out=rows[:, u, t * F:(t + 1) * F], out_offset=None, in_=table_d[:, :],
                                    in_offset=bass.IndirectOffsetOnAxis(ap=idx[:, u, t:t + 1], axis=0),
                                ).then_inc(rows_in[u], 16)

        @block.tensor
        def _(pe):
            pe.sem_inc(edge_w_free, 1)
            pe.sem_inc(node_w_free, 1)
            pe.sem_inc(gin_w_free, 1)
            for s in mm1_done + mm2_done + agg_done:
                pe.sem_inc(s, 1)
            pe.wait_ge(consts_in, 16 * 6)
            pe.wait_ge(consts_set, 5)
            K = load_passes(pe)

            def project(c, m, copied):
                pe.wait_ge(proj_copied, copied)
                for j in range(CH // P):
                    mm = pe.matmul(ps_t[c % 2][:, j * P:(j + 1) * P], hT[:, c * CH + j * P:c * CH + (j + 1) * P],
                                   m, start=True, stop=True)
                mm.then_inc(proj_done, 1)

            def aggregate(u, source, last, now):
                pe.wait_ge(hot_done[u], now)
                if u >= 2:
                    pe.wait_ge(add_done[u - 2], now)
                else:
                    pe.wait_ge(add_done[U - 2 + u], last)
                for t in range(TPG):
                    mm = pe.matmul(ps_a[u % 2][:, 0:WIN], source[:, t * F:(t + 1) * F], onehot[:, u % 2, t, :],
                                   start=(t == 0), stop=(t == TPG - 1))
                mm.then_inc(agg_done[u], 1)

            def node_product1(c, w, src, w_ready, src_sem, src_val):
                pe.wait_ge(src_sem, src_val)
                mm = pe.matmul(ps_h[c % 2][:, :], w, src, start=True, stop=True)
                mm.then_inc(n_prod1, 1)

            with pe.Fori(0, L0) as layer:
                pe.wait_ge(edge_w_in, layer * 32 + 32)
                for c in range(NCH):
                    pe.wait_ge(h_done, layer * NCH + NCH)
                    project(c, edge_w[:, EW_CW1:EW_CW1 + F], layer * NCH + c + 1)
                with pe.Fori(0, K) as k:
                    with pe.Fori(0, NIT) as it:
                        last = pe.snap(layer * (K * NIT) + k * NIT + it + 1)
                        now = pe.snap(last + 1)
                        landed = pe.snap(last * 16)
                        for i in range(U + 2):
                            if i < U:
                                pe.wait_ge(attr_in[i], landed)
                                if i >= 2:
                                    pe.wait_ge(ssp_done[i - 2], now)
                                else:
                                    pe.wait_ge(ssp_done[U - 2 + i], last)
                                pe.matmul(ps_h[i % 2][:, :], edge_w[0:G, EW_W1:EW_W1 + F], attr[:, i, :],
                                          start=True, stop=True).then_inc(mm1_done[i], 1)
                            if 1 <= i <= U:
                                u = i - 1
                                pe.wait_ge(ssp_done[u], now)
                                if u >= 2:
                                    pe.wait_ge(msg_done[u - 2], now)
                                else:
                                    pe.wait_ge(msg_done[U - 2 + u], last)
                                pe.matmul(ps_w[u % 2][:, :], ones_row[:, :], b2_row[:, :], start=True, stop=False)
                                for t in range(TPG):
                                    mm = pe.matmul(ps_w[u % 2][:, t * F:(t + 1) * F], hid[:, u % 2, t * P:(t + 1) * P],
                                                   edge_w[:, EW_W2:EW_W2 + F], start=False, stop=(t == TPG - 1))
                                mm.then_inc(mm2_done[u], 1)
                            if i >= 2:
                                u = i - 2
                                pe.wait_ge(msg_done[u], now)
                                aggregate(u, msg[:, u % 2, :], last, now)
                pe.sem_inc(edge_w_free, 1)
                pe.wait_ge(node_w_in, layer * 16 + 16)
                pe.wait_ge(add_done[U - 1], (layer + 1) * (K * NIT) + 1)
                for c in range(NCH + 1):
                    if c < NCH:
                        if c >= 2:
                            pe.wait_ge(n_ssp, layer * NCH + c - 1)
                        pe.matmul(ps_h[c % 2][:, :], node_w[:, NW_CW2:NW_CW2 + F], col(aggT, c),
                                  start=True, stop=True).then_inc(n_prod1, 1)
                    if c >= 1:
                        d = c - 1
                        pe.wait_ge(n_ssp, layer * NCH + d + 1)
                        if d >= 2:
                            pe.wait_ge(h_done, layer * NCH + NCH + d - 1)
                        pe.matmul(ps_w[d % 2][:, :], node_w[:, NW_LIN:NW_LIN + F], hid[:, d % 2, :],
                                  start=True, stop=True).then_inc(n_prod2, 1)

            def layer_norm(r):
                for c in range(NCH + 1):
                    if c < NCH:
                        pe.wait_ge(ln_sum, r * NCH + c + 1)
                        if c >= 2:
                            pe.wait_ge(ln_dev, r * NCH + c - 1)
                        pe.matmul(ps_h[c % 2][:, :], mean_mat[:, :], col(hT, c), start=True, stop=True
                                  ).then_inc(ln_mean, 1)
                    if c >= 1:
                        d = c - 1
                        pe.wait_ge(ln_sq, r * NCH + d + 1)
                        if d >= 2:
                            pe.wait_ge(ln_std, r * NCH + d - 1)
                        pe.matmul(ps_w[d % 2][:, :], mean_mat[:, :], lg[:, d % 2, :], start=True, stop=True
                                  ).then_inc(ln_var, 1)

            layer_norm(0)
            pe.wait_ge(ln_done, NCH)
            with pe.Fori(0, L1) as g:
                pe.wait_ge(gin_w_in, g * 16 + 16)
                for c in range(NCH):
                    pe.wait_ge(h_done, g * NCH + (L0 + 1) * NCH)
                    project(c, ident[:, :], g * NCH + L0 * NCH + c + 1)
                with pe.Fori(0, K) as k:
                    with pe.Fori(0, NIT) as it:
                        last = pe.snap((g + L0) * (K * NIT) + k * NIT + it + 1)
                        now = pe.snap(last + 1)
                        landed = pe.snap(last * (16 * TPG))
                        for u in range(U):
                            pe.wait_ge(rows_in[u], landed)
                            aggregate(u, rows[:, u, :], last, now)
                for c in range(NCH + 1):
                    if c < NCH:
                        pe.wait_ge(z_done, g * NCH + c + 1)
                        if c >= 2:
                            pe.wait_ge(n_act, (g + L0) * NCH + c - 1)
                        pe.matmul(ps_h[c % 2][:, :], gin_w[:, GW_W1:GW_W1 + F], xc[:, c % 2, :],
                                  start=True, stop=True).then_inc(n_prod1, 1)
                    if c >= 1:
                        d = c - 1
                        pe.wait_ge(n_act, (g + L0) * NCH + d + 1)
                        if d >= 2:
                            pe.wait_ge(h_done, (g + L0) * NCH + NCH + d - 1)
                        pe.matmul(ps_w[d % 2][:, :], gin_w[:, GW_W2:GW_W2 + F], hid[:, d % 2, :],
                                  start=True, stop=True).then_inc(n_prod2, 1)
            layer_norm(1)
            for c in range(NCH):
                pe.wait_ge(ln_done, NCH + c + 1)
                project(c, ident[:, :], (L0 + L1) * NCH + c + 1)

        @block.scalar
        def _(act):
            act.sem_inc(proj_copied, 2)
            for s in log_done:
                act.sem_inc(s, 1)
            act.wait_ge(consts_set, 5)
            act.wait_ge(pre, 4)
            act.activation(cut[:, :], cut[:, :], ACT.Sin, bias=half_pi[:, :], scale=-math.pi / CUTOFF
                           ).then_inc(cosine_done, 1)
            K = load_passes(act)

            def project(layer):
                for c in range(NCH):
                    act.wait_ge(proj_done, layer * NCH + c + 1)
                    act.copy(stage[:, c, :], ps_t[c % 2][:, :]).then_inc(proj_copied, 1)
                    act.wait_ge(proj_copied, layer * NCH + c + 3)
                    act.dma_start(table_rows[c], stage[:, c, :].rearrange("p (j f) -> p j f", f=F)
                                  ).then_inc(table_in[c], 16)

            with act.Fori(0, L0) as layer:
                project(layer)
                with act.Fori(0, K) as k:
                    with act.Fori(0, NIT) as it:
                        first = act.snap(layer * (K * NIT) + k * NIT + it)
                        now = act.snap(first + 2)
                        exps = act.snap(first * U)
                        for u in range(U):
                            act.wait_ge(clamp_done[u], now)
                            act.activation(ex[:, u % 2, :], xc[:, u % 2, :], ACT.Exp).then_inc(exp_done, 1)
                            act.wait_ge(exp_done, exps + (u + 1))
                            act.activation(lg[:, u % 2, :], ex[:, u % 2, :], ACT.Ln, bias=half[:, :], scale=0.5
                                           ).then_inc(log_done[u], 1)
                for c in range(NCH):
                    act.wait_ge(n_clamp, layer * NCH + c + 1)
                    act.activation(ex[:, c % 2, :], xc[:, c % 2, :], ACT.Exp).then_inc(n_exp, 1)
                    act.wait_ge(n_exp, layer * NCH + c + 1)
                    act.activation(lg[:, c % 2, :], ex[:, c % 2, :], ACT.Ln, bias=half[:, :], scale=0.5
                                   ).then_inc(n_act, 1)

            def layer_norm(r):
                for c in range(NCH + 1):
                    if c < NCH:
                        act.wait_ge(ln_dev, r * NCH + c + 1)
                        if c >= 2:
                            act.wait_ge(ln_var, r * NCH + c - 1)
                        act.activation(lg[:, c % 2, :], col(hT, c), ACT.Square).then_inc(ln_sq, 1)
                    if c >= 1:
                        d = c - 1
                        act.wait_ge(ln_var, r * NCH + d + 1)
                        if d >= 2:
                            act.wait_ge(ln_done, r * NCH + d - 1)
                        act.activation(ex[:, d % 2, :], ps_w[d % 2][:, :], ACT.Sqrt, bias=eps_col[:, :]
                                       ).then_inc(ln_std, 1)

            layer_norm(0)
            with act.Fori(0, L1) as g:
                project(g + L0)
                act.wait_ge(gin_w_in, g * 16 + 16)
                for c in range(NCH):
                    act.wait_ge(n_prod1, (g + L0) * NCH + c + 1)
                    if c >= 2:
                        act.wait_ge(n_prod2, (g + L0) * NCH + c - 1)
                    act.activation(hid[:, c % 2, :], ps_h[c % 2][:, :], ACT.Relu,
                                   bias=gin_w[:, GW_B1:GW_B1 + 1]).then_inc(n_act, 1)
            layer_norm(1)
            for c in range(NCH):
                done = (L0 + L1) * NCH + c
                act.wait_ge(proj_done, done + 1)
                act.copy(stage[:, c, :], ps_t[c % 2][:, :]).then_inc(proj_copied, 1)
                act.wait_ge(proj_copied, done + 3)
                full = min((N - c * CH) // P, CH // P)
                act.dma_start(out_d[c * CH:c * CH + full * P, :].rearrange("(j p) f -> p j f", p=P),
                              stage[:, c, 0:full * F].rearrange("p (j f) -> p j f", f=F)).then_inc(out_done, 16)
                rest = min(N - c * CH, CH) - full * P
                if rest:
                    act.dma_start(out_d[c * CH + full * P:N, :], stage[0:rest, c, full * F:(full + 1) * F]
                                  ).then_inc(out_done, 16)
            act.wait_ge(out_done, 16 * (NCH + (1 if N % P else 0)))

        @block.vector
        def _(dve):
            for s in clamp_done + ssp_done + msg_done + hot_done + add_done:
                dve.sem_inc(s, 1)
            dve.wait_ge(consts_in, 16 * 6)
            dst_f = rel
            dve.tensor_copy(dst_f[:, :], dst_i[:, :]).then_inc(pre, 1)
            dve.wait_ge(pre, 1)
            grouped = dst_f[:, :].rearrange("p (g t) -> p g t", t=TPG)
            dve.tensor_reduce(base_f[:, :], grouped, AX.X, ALU.min)
            dve.tensor_reduce(ends[:, 1, :], grouped, AX.X, ALU.max).then_inc(pre, 1)
            dve.wait_ge(pre, 2)
            dve.tensor_scalar(ends[:, 0, :], base_f[:, :], -1.0, None, ALU.mult).then_inc(pre, 1)
            dve.tensor_scalar(cut[:, :], len_raw[:, :], 0.0, CUTOFF, ALU.max, ALU.min).then_inc(pre, 1)
            dve.tensor_scalar(len_mask[:, :], len_raw[:, :], 0.0, None, ALU.is_ge).then_inc(pre, 1)
            dve.wait_ge(pre, 5)
            dve.scalar_tensor_tensor(out=len_raw[:, :], in0=len_raw[:, :], scalar=CUTOFF, in1=len_mask[:, :],
                                     op0=ALU.is_le, op1=ALU.mult).then_inc(pre, 1)
            dve.wait_ge(cosine_done, 1)
            dve.tensor_scalar(cut[:, :], cut[:, :], 1.0, 0.5, ALU.add, ALU.mult).then_inc(pre, 1)
            dve.wait_ge(pre, 7)
            dve.tensor_tensor(cut[:, :], cut[:, :], len_raw[:, :], ALU.mult).then_inc(pre, 1)
            dve.wait_ge(ends_reduced, 1)
            dve.tensor_scalar(base_f[:, :], ends_all[:, 0, :], -1.0, None, ALU.mult).then_inc(pre, 1)
            dve.tensor_tensor(span[:, :], ends_all[:, 0, :], ends_all[:, 1, :], ALU.add).then_inc(pre, 1)
            dve.wait_ge(pre, 10)
            dve.tensor_copy(base_i[:, :], base_f[:, :]).then_inc(pre, 1)
            dve.tensor_tensor(grouped, grouped, base_f[:, :].unsqueeze(2).broadcast_to([P, NG, TPG]),
                              ALU.subtract).then_inc(pre, 1)
            dve.tensor_reduce(span_max[:, :], span[:, :], AX.X, ALU.max).then_inc(pre, 1)
            dve.wait_ge(pre, 13)
            dve.tensor_copy(span_i[:, :], span_max[:, :]).then_inc(pre, 1)
            dve.wait_ge(pre, 14)
            dve.tensor_scalar(span_s[:, :], span_i[:, :], WIN.bit_length() - 1, None, ALU.arith_shift_right
                              ).then_inc(pre, 1)
            dve.wait_ge(pre, 15)
            dve.tensor_scalar(passes[:, :], span_s[:, :], 1.0, None, ALU.add).then_inc(pre, 1)
            dve.memset(aggT[:, :], 0.0).then_inc(agg_clear, 1)
            dve.wait_ge(pre, 16)
            dve.wait_ge(agg_clear, 1)
            dve.sem_inc(h_done, NCH)
            dve.sem_inc(ready, 1)
            K = load_passes(dve)

            def one_hot(u, last, now, factor):
                for t in range(TPG):
                    j = u * TPG + t
                    if factor:
                        op = dve.tensor_scalar(onehot[:, u % 2, t, :], win_now[:, :], rel_now[:, j:j + 1],
                                               cut_now[:, j:j + 1], ALU.is_equal, ALU.mult)
                    else:
                        op = dve.tensor_scalar(onehot[:, u % 2, t, :], win_now[:, :], rel_now[:, j:j + 1],
                                               None, ALU.is_equal)
                op.then_inc(hot_done[u], 1)

            def add_window(u, it, k, last, now):
                start = dve.value_load(base_i[0:1, bass.ds(it * U + u, 1)], min_val=0, max_val=N)
                window = aggT[:, bass.ds(start + k * WIN, WIN)]
                dve.wait_ge(agg_done[u], now)
                if u:
                    dve.wait_ge(add_done[u - 1], now)
                else:
                    dve.wait_ge(add_done[U - 1], last)
                dve.tensor_tensor(window, window, ps_a[u % 2][:, 0:WIN], ALU.add).then_inc(add_done[u], 1)

            def iteration_slices(it, n):
                dve.tensor_copy(rel_now[:, :], rel[:, bass.ds(it * (U * TPG), U * TPG)]).then_inc(slices_set, 1)
                dve.tensor_copy(cut_now[:, :], cut[:, bass.ds(it * (U * TPG), U * TPG)]).then_inc(slices_set, 1)
                dve.wait_ge(slices_set, n * 2 + 2)

            with dve.Fori(0, L0) as layer:
                dve.wait_ge(edge_w_in, layer * 32 + 32)
                dve.tensor_scalar(b1_ln2[:, :], edge_w[:, EW_B1:EW_B1 + 1], -LN2, None, ALU.add).then_inc(b1_set, 1)
                with dve.Fori(0, K) as k:
                    dve.wait_ge(b1_set, layer + 1)
                    dve.wait_ge(agg_clear, layer + 1)
                    dve.tensor_copy(win_now[:, :], iota[:, bass.ds(k * WIN, WIN)]).then_inc(win_set, 1)
                    with dve.Fori(0, NIT) as it:
                        n = dve.snap(layer * (K * NIT) + k * NIT + it)
                        dve.wait_ge(win_set, layer * K + k + 1)
                        last = dve.snap(n + 1)
                        now = dve.snap(n + 2)
                        landed = dve.snap(last * (16 * TPG))
                        iteration_slices(it, n)
                        for i in range(U + 3):
                            if i < U:
                                dve.wait_ge(mm1_done[i], now)
                                dve.tensor_scalar(xc[:, i % 2, :], ps_h[i % 2][:, :], edge_w[:, EW_B1:EW_B1 + 1],
                                                  XCLAMP, ALU.add, ALU.min).then_inc(clamp_done[i], 1)
                            if 1 <= i <= U:
                                u = i - 1
                                dve.wait_ge(log_done[u], now)
                                dve.scalar_tensor_tensor(out=hid[:, u % 2, :], in0=ps_h[u % 2][:, :],
                                                         scalar=b1_ln2[:, :], in1=lg[:, u % 2, :],
                                                         op0=ALU.add, op1=ALU.max).then_inc(ssp_done[u], 1)
                            if 2 <= i <= U + 1:
                                u = i - 2
                                one_hot(u, last, now, True)
                                dve.wait_ge(mm2_done[u], now)
                                dve.wait_ge(rows_in[u], landed)
                                dve.tensor_tensor(msg[:, u % 2, :], ps_w[u % 2][:, :], rows[:, u, :], ALU.mult
                                                  ).then_inc(msg_done[u], 1)
                            if i >= 3:
                                add_window(i - 3, it, k, last, now)
                dve.wait_ge(node_w_in, layer * 16 + 16)
                dve.tensor_scalar(cb2_ln2[:, :], node_w[:, NW_CB2:NW_CB2 + 1], -LN2, None, ALU.add
                                  ).then_inc(cb2_set, 1)
                dve.wait_ge(cb2_set, layer + 1)
                for c in range(NCH + 2):
                    if c < NCH:
                        dve.wait_ge(n_prod1, layer * NCH + c + 1)
                        dve.tensor_scalar(xc[:, c % 2, :], ps_h[c % 2][:, :], node_w[:, NW_CB2:NW_CB2 + 1],
                                          XCLAMP, ALU.add, ALU.min).then_inc(n_clamp, 1)
                    if 1 <= c <= NCH:
                        d = c - 1
                        dve.wait_ge(n_act, layer * NCH + d + 1)
                        dve.scalar_tensor_tensor(out=hid[:, d % 2, :], in0=ps_h[d % 2][:, :], scalar=cb2_ln2[:, :],
                                                 in1=lg[:, d % 2, :], op0=ALU.add, op1=ALU.max).then_inc(n_ssp, 1)
                    if c >= 2:
                        d = c - 2
                        dve.wait_ge(n_prod2, layer * NCH + d + 1)
                        dve.scalar_tensor_tensor(out=col(hT, d), in0=ps_w[d % 2][:, :],
                                                 scalar=node_w[:, NW_LB:NW_LB + 1], in1=col(hT, d),
                                                 op0=ALU.add, op1=ALU.add).then_inc(h_done, 1)
                dve.wait_ge(h_done, layer * NCH + 2 * NCH)
                dve.sem_inc(node_w_free, 1)
                dve.memset(aggT[:, :], 0.0).then_inc(agg_clear, 1)

            def layer_norm(r, keep):
                for c in range(NCH):
                    dve.tensor_tensor(col(hT, c), col(hT, c), col(xT, c), ALU.add).then_inc(ln_sum, 1)
                for c in range(NCH + 2):
                    if c < NCH:
                        dve.wait_ge(ln_mean, r * NCH + c + 1)
                        dve.tensor_tensor(col(hT, c), col(hT, c), ps_h[c % 2][:, :], ALU.subtract
                                          ).then_inc(ln_dev, 1)
                    if c >= 2:
                        d = c - 2
                        dve.wait_ge(ln_std, r * NCH + d + 1)
                        dve.reciprocal(ex[:, d % 2, :], ex[:, d % 2, :]).then_inc(ln_inv, 1)
                        dve.wait_ge(ln_inv, r * NCH + d + 1)
                        dve.tensor_tensor(col(hT, d), col(hT, d), ex[:, d % 2, :], ALU.mult).then_inc(ln_done, 1)
                        if keep:
                            dve.wait_ge(ln_done, r * NCH + d + 1)
                            dve.tensor_copy(col(xT, d), col(hT, d)).then_inc(ln_keep, 1)

            layer_norm(0, True)
            dve.wait_ge(ln_keep, NCH)
            with dve.Fori(0, L1) as g:
                dve.wait_ge(gin_w_in, g * 16 + 16)
                dve.tensor_scalar(eps1[:, :], gin_w[:, GW_EPS:GW_EPS + 1], 1.0, None, ALU.add).then_inc(eps1_set, 1)
                with dve.Fori(0, K) as k:
                    dve.wait_ge(eps1_set, g + 1)
                    dve.wait_ge(agg_clear, g + (L0 + 1))
                    dve.tensor_copy(win_now[:, :], iota[:, bass.ds(k * WIN, WIN)]).then_inc(win_set, 1)
                    with dve.Fori(0, NIT) as it:
                        n = dve.snap((g + L0) * (K * NIT) + k * NIT + it)
                        dve.wait_ge(win_set, (g + L0) * K + k + 1)
                        last = dve.snap(n + 1)
                        now = dve.snap(n + 2)
                        iteration_slices(it, n)
                        for i in range(U + 1):
                            if i < U:
                                one_hot(i, last, now, False)
                            if i >= 1:
                                add_window(i - 1, it, k, last, now)
                                dve.sem_inc(msg_done[i - 1], 1)
                for c in range(NCH + 2):
                    if c < NCH:
                        if c >= 2:
                            dve.wait_ge(n_prod1, (g + L0) * NCH + c - 1)
                        dve.scalar_tensor_tensor(out=xc[:, c % 2, :], in0=col(hT, c), scalar=eps1[:, :],
                                                 in1=col(aggT, c), op0=ALU.mult, op1=ALU.add).then_inc(z_done, 1)
                    if c >= 2:
                        d = c - 2
                        dve.wait_ge(n_prod2, (g + L0) * NCH + d + 1)
                        dve.tensor_scalar(col(hT, d), ps_w[d % 2][:, :], gin_w[:, GW_B2:GW_B2 + 1], None, ALU.add
                                          ).then_inc(h_done, 1)
                dve.wait_ge(h_done, (g + L0 + 2) * NCH)
                dve.sem_inc(gin_w_free, 1)
                dve.memset(aggT[:, :], 0.0).then_inc(agg_clear, 1)
            layer_norm(1, False)


def kernel(x, src, dst, edge_attr_100, edge_weight, L0_gnn_mlp_w1, L0_gnn_mlp_b1, L0_gnn_mlp_w2, L0_gnn_mlp_b2,
           L0_gnn_conv_w1, L0_gnn_conv_w2, L0_gnn_conv_b2, L0_gnn_lin_w, L0_gnn_lin_b,
           L1_gnn_W1, L1_gnn_b1, L1_gnn_W2, L1_gnn_b2, L1_gnn_eps):
    import numpy as np
    import concourse.bacc as bacc
    from concourse.bass_utils import run_bass_kernel_spmd

    def arr(a):
        return np.asarray(a)

    def padded(a, n, value=0):
        return np.concatenate([a, np.full((n - a.shape[0],) + a.shape[1:], value, a.dtype)])

    def by_column(a):
        return np.ascontiguousarray(a.reshape(NG * TPG, P).T)

    xT = np.ascontiguousarray(padded(arr(x), NP).T)
    src_g = np.ascontiguousarray(padded(arr(src), EP).reshape(NG, TPG, P).transpose(0, 2, 1))
    dst_c = by_column(padded(arr(dst), EP, N))
    ew_c = by_column(padded(arr(edge_weight), EP))
    attr = np.ascontiguousarray(padded(arr(edge_attr_100), EP).reshape(NG, GE, G).transpose(0, 2, 1))
    w1 = np.zeros((L0, P, F), np.float32)
    w1[:, :G] = arr(L0_gnn_mlp_w1)
    edge_w = np.concatenate([w1, arr(L0_gnn_mlp_w2), arr(L0_gnn_conv_w1), arr(L0_gnn_mlp_b1)[:, :, None]], axis=2)
    b2_row = np.ascontiguousarray(np.tile(arr(L0_gnn_mlp_b2), (1, TPG))[:, None, :])
    node_w = np.concatenate([arr(L0_gnn_conv_w2), arr(L0_gnn_lin_w), arr(L0_gnn_conv_b2)[:, :, None],
                             arr(L0_gnn_lin_b)[:, :, None]], axis=2)
    eps = np.ascontiguousarray(np.broadcast_to(arr(L1_gnn_eps)[:, None, None], (L1, P, 1)))
    gin_w = np.concatenate([arr(L1_gnn_W1), arr(L1_gnn_W2), arr(L1_gnn_b1)[:, :, None],
                            arr(L1_gnn_b2)[:, :, None], eps], axis=2)
    ident = np.eye(P, dtype=np.float32)
    iota = np.ascontiguousarray(np.broadcast_to(np.arange(KMAX * WIN, dtype=np.float32), (P, KMAX * WIN)))

    nc = bacc.Bacc("TRN2", target_bir_lowering=False, num_devices=1)
    arrays, args = {}, []
    for name, a in (("xT", xT), ("src", src_g), ("dst", dst_c), ("edge_len", ew_c), ("attr", attr),
                    ("edge_w", edge_w), ("b2_row", b2_row), ("node_w", node_w), ("gin_w", gin_w),
                    ("ident", ident), ("iota", iota)):
        arrays[f"in_{name}"] = a
        args.append(nc.dram_tensor(f"in_{name}", a.shape, mybir.dt.from_np(a.dtype), kind="ExternalInput").ap())
    out = nc.dram_tensor("out", (N, F), mybir.dt.float32, kind="ExternalOutput").ap()
    gnn_program(nc, *args, out)
    return run_bass_kernel_spmd(nc, [arrays], core_ids=[0]).results[0]["out"]
```

```python
import concourse.bass as bass
from concourse import mybir
from contextlib import ExitStack
import math

P = 128
N = 2500
E = 82500
F = 128
G = 100
L0 = 6
L1 = 3
TPG = 4
GE = TPG * P
S = 6
U = 18
Q = U // S
NG = -(-E // GE)
NIT = NG // U
assert NG % U == 0 and U % S == 0
EP = NG * GE
WIN = 32
KMAX = N // WIN + 1
CH = 512
NCH = -(-N // CH)
NP = NCH * CH
AGW = N + (KMAX + 1) * WIN
CUTOFF = 10.0
LN2 = math.log(2.0)
XCLAMP = 40.0
LN_EPS = 1e-5

EW_W1, EW_W2, EW_CW1, EW_B1, EW_N = 0, F, 2 * F, 3 * F, 3 * F + 1
NW_CW2, NW_LIN, NW_CB2, NW_LB, NW_N = 0, F, 2 * F, 2 * F + 1, 2 * F + 2
GW_W1, GW_W2, GW_B1, GW_B2, GW_EPS, GW_N = 0, F, 2 * F, 2 * F + 1, 2 * F + 2, 2 * F + 3


def gnn_program(nc, xT_d, src_d, dst_d, ew_d, attr_d, edge_w_d, b2_d, node_w_d, gin_w_d, ident_d, iota_d, out_d):
    f32, i32, bf16 = mybir.dt.float32, mybir.dt.int32, mybir.dt.bfloat16
    ACT, ALU, AX = mybir.ActivationFunctionType, mybir.AluOpType, mybir.AxisListType
    RMAX = bass.bass_isa.ReduceOp.max
    table_d = nc.dram_tensor("node_table", [NP, F], f32, kind="Internal").ap()

    with ExitStack() as ctx:
        def sb(name, shape, dt=f32):
            return ctx.enter_context(nc.sbuf_tensor(name, shape, dt))

        def psum(name, n):
            return [ctx.enter_context(nc.psum_tensor(f"{name}{i}", [P, 512], f32)) for i in range(n)]

        def sem(name):
            return ctx.enter_context(nc.semaphore(name))

        def slot_sems(name, n=S):
            return [sem(f"{name}{i}") for i in range(n)]

        xT = sb("xT", [P, NP])
        hT = sb("hT", [P, NP])
        aggT = sb("aggT", [P, AGW])
        stage = sb("stage", [P, NCH, CH])
        ident = sb("ident", [P, P])
        mean_mat = sb("mean_mat", [P, P])
        ones3 = sb("ones3", [3, P], bf16)
        iota = sb("iota", [P, KMAX * WIN])
        half = sb("half", [P, 1])
        half_pi = sb("half_pi", [P, 1])
        eps_col = sb("eps_col", [P, 1])

        edge_w = sb("edge_w", [P, EW_N])
        b1_ln2 = sb("b1_ln2", [P, 1])
        b2_row = sb("b2_row", [1, GE])
        b2_rest = sb("b2_rest", [1, 2, GE])
        b2_flat = sb("b2_flat", [1, 3, GE], bf16)
        b2_parts = sb("b2_parts", [3, GE], bf16)
        node_w = sb("node_w", [P, NW_N])
        cb2_ln2 = sb("cb2_ln2", [P, 1])
        gin_w = sb("gin_w", [P, GW_N])
        eps1 = sb("eps1", [P, 1])
        dst_i = sb("dst_i", [P, NG * TPG], i32)
        rel = sb("rel", [P, NG * TPG])
        cut = sb("cut", [P, NG * TPG])
        len_raw = sb("len_raw", [P, NG * TPG])
        len_mask = sb("len_mask", [P, NG * TPG])
        ends = sb("ends", [P, 2, NG])
        ends_all = sb("ends_all", [P, 2, NG])
        base_f = sb("base_f", [P, NG])
        base_i = sb("base_i", [P, NG], i32)
        span = sb("span", [P, NG])
        span_max = sb("span_max", [P, 1])
        span_i = sb("span_i", [P, 1], i32)
        span_s = sb("span_s", [P, 1], i32)
        passes = sb("passes", [P, 1], i32)
        attr = sb("attr", [G, S, GE])
        idx = sb("idx", [P, S, TPG], i32)
        rows = sb("rows", [P, S, GE])
        rel_now = sb("rel_now", [P, U * TPG])
        cut_now = sb("cut_now", [P, U * TPG])
        win_now = sb("win_now", [P, WIN])
        xc = sb("xc", [P, 2, GE])
        ex = sb("ex", [P, 2, GE])
        lg = sb("lg", [P, 2, GE])
        hid = sb("hid", [P, 3, GE])
        msg = sb("msg", [P, 3, GE])
        onehot = sb("onehot", [P, 3, TPG, WIN])

        ps_h, ps_w, ps_a, ps_t = (psum(name, 2) for name in ("ps_h", "ps_w", "ps_a", "ps_t"))

        consts_in, consts_set = sem("consts_in"), sem("consts_set")
        pre = sem("pre")
        ends_reduced, cosine_done, ready = sem("ends_reduced"), sem("cosine_done"), sem("ready")
        edge_w_in, node_w_in, gin_w_in = sem("edge_w_in"), sem("node_w_in"), sem("gin_w_in")
        b2_split, b2_in = sem("b2_split"), sem("b2_in")
        edge_w_free, node_w_free, gin_w_free = sem("edge_w_free"), sem("node_w_free"), sem("gin_w_free")
        b1_set, cb2_set, eps1_set = sem("b1_set"), sem("cb2_set"), sem("eps1_set")
        table_in = slot_sems("table_in", NCH)
        attr_in, idx_in, rows_in = slot_sems("attr_in"), slot_sems("idx_in"), slot_sems("rows_in")
        mm1_done, clamp_done, log_done, ssp_done = (slot_sems(s) for s in ("mm1_", "clamp_", "log_", "ssp_"))
        mm2_done, msg_done, hot_done, agg_done, add_done = (slot_sems(s) for s in
                                                            ("mm2_", "msg_", "hot_", "agg_", "add_"))
        exp_done = slot_sems("exp_")
        slices_set, win_set = sem("slices_set"), sem("win_set")
        proj_done, proj_copied = sem("proj_done"), sem("proj_copied")
        n_prod1, n_clamp, n_exp, n_act, n_ssp, n_prod2 = (sem(s) for s in
            ("n_prod1", "n_clamp", "n_exp", "n_act", "n_ssp", "n_prod2"))
        h_done, agg_clear, z_done = sem("h_done"), sem("agg_clear"), sem("z_done")
        ln_sum, ln_mean, ln_dev, ln_sq, ln_var, ln_std, ln_inv, ln_done, ln_keep = (sem(s) for s in
            ("ln_sum", "ln_mean", "ln_dev", "ln_sq", "ln_var", "ln_std", "ln_inv", "ln_done", "ln_keep"))
        out_done = sem("out_done")
        gate = sem("gate")

        table_rows = table_d.rearrange("(c j p) f -> c p j f", j=CH // P, p=P)

        def load_passes(eng):
            eng.wait_ge(ready, 1)
            return eng.value_load(passes[0:1, 0:1], min_val=1, max_val=KMAX)

        class Uses:

            def __init__(self, eng, n):
                self.eng, self.n, self.regs = eng, n, {}

            def value(self, u, scale=1, prime=1):
                key = (u // S + prime, scale)
                if key not in self.regs:
                    self.regs[key] = self.eng.snap((self.n * Q + (key[0] + 1)) * scale)
                return self.regs[key]

            def wait(self, sems, u):
                self.eng.wait_ge(sems[u % S], self.value(u))

            def wait_dma(self, sems, u, dmas=1):
                self.eng.wait_ge(sems[u % S], self.value(u, 16 * dmas, 0))

        def col(t, c):
            return t[:, c * CH:(c + 1) * CH]

        block = ctx.enter_context(nc.Block())

        @block.sync
        def _(sp):
            for t, s in ((dst_i, dst_d), (len_raw, ew_d), (xT, xT_d), (hT, xT_d), (ident, ident_d), (iota, iota_d)):
                sp.dma_start(t[:, :], s).then_inc(consts_in, 16)
            K = load_passes(sp)

            def edge_loads(layer, with_attr):
                with sp.Fori(0, K) as k:
                    with sp.Fori(0, NIT) as it:
                        uses = Uses(sp, layer * (K * NIT) + k * NIT + it)
                        for u in range(U):
                            g = it * U + u
                            uses.wait(msg_done, u - S)
                            sp.dma_start(idx[:, u % S, :], src_d[bass.ds(g, 1)].rearrange("a p t -> (a p) t")
                                         ).then_inc(idx_in[u % S], 16)
                            if with_attr:
                                uses.wait(mm1_done, u - S)
                                sp.dma_start(attr[:, u % S, :], attr_d[bass.ds(g, 1)].rearrange("a p t -> (a p) t")
                                             ).then_inc(attr_in[u % S], 16)

            with sp.Fori(0, L0) as layer:
                sp.wait_ge(edge_w_free, layer + 1)
                sp.dma_start(edge_w[:, :], edge_w_d[bass.ds(layer, 1)].rearrange("a p t -> (a p) t")
                             ).then_inc(edge_w_in, 16)
                sp.dma_start(b2_row[:, :], b2_d[bass.ds(layer, 1)].rearrange("a p t -> (a p) t")
                             ).then_inc(edge_w_in, 16)
                sp.wait_ge(b2_split, layer * 5 + 5)
                sp.dma_start(b2_parts[:, :], b2_flat[0:1, :, :]
                             ).then_inc(b2_in, 16)
                sp.wait_ge(node_w_free, layer + 1)
                sp.dma_start(node_w[:, :], node_w_d[bass.ds(layer, 1)].rearrange("a p t -> (a p) t")
                             ).then_inc(node_w_in, 16)
                edge_loads(layer, True)
            with sp.Fori(0, L1) as g:
                sp.wait_ge(gin_w_free, g + 1)
                sp.dma_start(gin_w[:, :], gin_w_d[bass.ds(g, 1)].rearrange("a p t -> (a p) t")
                             ).then_inc(gin_w_in, 16)
                edge_loads(L0 + g, False)

        @block.gpsimd
        def _(pool):
            pool.memset(mean_mat[:, :], 1.0 / F).then_inc(consts_set, 1)
            pool.memset(ones3[:, :], 1.0).then_inc(consts_set, 1)
            pool.memset(half[:, :], 0.5).then_inc(consts_set, 1)
            pool.memset(half_pi[:, :], math.pi / 2).then_inc(consts_set, 1)
            pool.memset(eps_col[:, :], LN_EPS).then_inc(consts_set, 1)
            pool.wait_ge(pre, 3)
            pool.partition_all_reduce(ends_all[:, :, :].rearrange("p a g -> p (a g)"),
                                      ends[:, :, :].rearrange("p a g -> p (a g)"), P, RMAX).then_inc(ends_reduced, 1)
            K = load_passes(pool)
            with pool.Fori(0, L0 + L1) as layer:
                for c in range(NCH):
                    pool.wait_ge(table_in[c], layer * 16 + 16)
                    pool.sem_inc(gate, 1)
                with pool.Fori(0, K) as k:
                    with pool.Fori(0, NIT) as it:
                        uses = Uses(pool, layer * (K * NIT) + k * NIT + it)
                        for u in range(U):
                            uses.wait_dma(idx_in, u)
                            uses.wait(msg_done, u - S)
                            pool.sem_inc(gate, 1)
                            for t in range(TPG):
                                pool.indirect_dma_start(
                                    out=rows[:, u % S, t * F:(t + 1) * F], out_offset=None, in_=table_d[:, :],
                                    in_offset=bass.IndirectOffsetOnAxis(ap=idx[:, u % S, t:t + 1], axis=0),
                                ).then_inc(rows_in[u % S], 16)

        @block.tensor
        def _(pe):
            pe.sem_inc(edge_w_free, 1)
            pe.sem_inc(node_w_free, 1)
            pe.sem_inc(gin_w_free, 1)
            for s in mm1_done + mm2_done + agg_done:
                pe.sem_inc(s, 1)
            pe.wait_ge(consts_in, 16 * 6)
            pe.wait_ge(consts_set, 5)
            K = load_passes(pe)

            def project(c, m, copied):
                pe.wait_ge(proj_copied, copied)
                for j in range(CH // P):
                    mm = pe.matmul(ps_t[c % 2][:, j * P:(j + 1) * P], hT[:, c * CH + j * P:c * CH + (j + 1) * P],
                                   m, start=True, stop=True)
                mm.then_inc(proj_done, 1)

            def aggregate(uses, u, source):
                uses.wait(hot_done, u)
                uses.wait(add_done, u - 2)
                for t in range(TPG):
                    mm = pe.matmul(ps_a[u % 2][:, 0:WIN], source[:, t * F:(t + 1) * F], onehot[:, u % 3, t, :],
                                   start=(t == 0), stop=(t == TPG - 1))
                mm.then_inc(agg_done[u % S], 1)

            def node_product1(c, w, src, w_ready, src_sem, src_val):
                pe.wait_ge(src_sem, src_val)
                mm = pe.matmul(ps_h[c % 2][:, :], w, src, start=True, stop=True)
                mm.then_inc(n_prod1, 1)

            with pe.Fori(0, L0) as layer:
                pe.wait_ge(edge_w_in, layer * 32 + 32)
                pe.wait_ge(b2_in, layer * 16 + 16)
                for c in range(NCH):
                    pe.wait_ge(h_done, layer * NCH + NCH)
                    project(c, edge_w[:, EW_CW1:EW_CW1 + F], layer * NCH + c + 1)
                with pe.Fori(0, K) as k:
                    with pe.Fori(0, NIT) as it:
                        uses = Uses(pe, layer * (K * NIT) + k * NIT + it)
                        for i in range(U + 4):
                            if i < U:
                                uses.wait_dma(attr_in, i)
                                uses.wait(ssp_done, i - 2)
                                pe.matmul(ps_h[i % 2][:, :], edge_w[0:G, EW_W1:EW_W1 + F], attr[:, i % S, :],
                                          start=True, stop=True).then_inc(mm1_done[i % S], 1)
                            u = i - 2
                            if 0 <= u < U:
                                uses.wait(ssp_done, u)
                                uses.wait(msg_done, u - 2)
                                pe.matmul(ps_w[u % 2][:, :], ones3[:, :], b2_parts[:, :], start=True, stop=False)
                                for t in range(TPG):
                                    mm = pe.matmul(ps_w[u % 2][:, t * F:(t + 1) * F], hid[:, u % 3, t * P:(t + 1) * P],
                                                   edge_w[:, EW_W2:EW_W2 + F], start=False, stop=(t == TPG - 1))
                                mm.then_inc(mm2_done[u % S], 1)
                            u = i - 4
                            if u >= 0:
                                uses.wait(msg_done, u)
                                aggregate(uses, u, msg[:, u % 3, :])
                pe.sem_inc(edge_w_free, 1)
                pe.wait_ge(node_w_in, layer * 16 + 16)
                pe.wait_ge(add_done[(U - 1) % S], (layer + 1) * (K * (NIT * Q)) + 1)
                for c in range(NCH + 1):
                    if c < NCH:
                        if c >= 2:
                            pe.wait_ge(n_ssp, layer * NCH + c - 1)
                        pe.matmul(ps_h[c % 2][:, :], node_w[:, NW_CW2:NW_CW2 + F], col(aggT, c),
                                  start=True, stop=True).then_inc(n_prod1, 1)
                    if c >= 1:
                        d = c - 1
                        pe.wait_ge(n_ssp, layer * NCH + d + 1)
                        if d >= 2:
                            pe.wait_ge(h_done, layer * NCH + NCH + d - 1)
                        pe.matmul(ps_w[d % 2][:, :], node_w[:, NW_LIN:NW_LIN + F], hid[:, d % 2, :],
                                  start=True, stop=True).then_inc(n_prod2, 1)

            def layer_norm(r):
                for c in range(NCH + 1):
                    if c < NCH:
                        pe.wait_ge(ln_sum, r * NCH + c + 1)
                        if c >= 2:
                            pe.wait_ge(ln_dev, r * NCH + c - 1)
                        pe.matmul(ps_h[c % 2][:, :], mean_mat[:, :], col(hT, c), start=True, stop=True
                                  ).then_inc(ln_mean, 1)
                    if c >= 1:
                        d = c - 1
                        pe.wait_ge(ln_sq, r * NCH + d + 1)
                        if d >= 2:
                            pe.wait_ge(ln_std, r * NCH + d - 1)
                        pe.matmul(ps_w[d % 2][:, :], mean_mat[:, :], lg[:, d % 2, :], start=True, stop=True
                                  ).then_inc(ln_var, 1)

            layer_norm(0)
            pe.wait_ge(ln_done, NCH)
            with pe.Fori(0, L1) as g:
                pe.wait_ge(gin_w_in, g * 16 + 16)
                for c in range(NCH):
                    pe.wait_ge(h_done, g * NCH + (L0 + 1) * NCH)
                    project(c, ident[:, :], g * NCH + L0 * NCH + c + 1)
                with pe.Fori(0, K) as k:
                    with pe.Fori(0, NIT) as it:
                        uses = Uses(pe, (g + L0) * (K * NIT) + k * NIT + it)
                        for u in range(U):
                            uses.wait_dma(rows_in, u, TPG)
                            aggregate(uses, u, rows[:, u % S, :])
                for c in range(NCH + 1):
                    if c < NCH:
                        pe.wait_ge(z_done, g * NCH + c + 1)
                        if c >= 2:
                            pe.wait_ge(n_act, (g + L0) * NCH + c - 1)
                        pe.matmul(ps_h[c % 2][:, :], gin_w[:, GW_W1:GW_W1 + F], xc[:, c % 2, :],
                                  start=True, stop=True).then_inc(n_prod1, 1)
                    if c >= 1:
                        d = c - 1
                        pe.wait_ge(n_act, (g + L0) * NCH + d + 1)
                        if d >= 2:
                            pe.wait_ge(h_done, (g + L0) * NCH + NCH + d - 1)
                        pe.matmul(ps_w[d % 2][:, :], gin_w[:, GW_W2:GW_W2 + F], hid[:, d % 2, :],
                                  start=True, stop=True).then_inc(n_prod2, 1)
            layer_norm(1)
            for c in range(NCH):
                pe.wait_ge(ln_done, NCH + c + 1)
                project(c, ident[:, :], (L0 + L1) * NCH + c + 1)

        @block.scalar
        def _(act):
            act.sem_inc(proj_copied, 2)
            for s in exp_done + log_done:
                act.sem_inc(s, 1)
            act.wait_ge(consts_set, 5)
            act.wait_ge(pre, 4)
            act.activation(cut[:, :], cut[:, :], ACT.Sin, bias=half_pi[:, :], scale=-math.pi / CUTOFF
                           ).then_inc(cosine_done, 1)
            K = load_passes(act)

            def project(layer):
                for c in range(NCH):
                    act.wait_ge(proj_done, layer * NCH + c + 1)
                    act.copy(stage[:, c, :], ps_t[c % 2][:, :]).then_inc(proj_copied, 1)
                    act.wait_ge(proj_copied, layer * NCH + c + 3)
                    act.dma_start(table_rows[c], stage[:, c, :].rearrange("p (j f) -> p j f", f=F)
                                  ).then_inc(table_in[c], 16)

            with act.Fori(0, L0) as layer:
                project(layer)
                with act.Fori(0, K) as k:
                    with act.Fori(0, NIT) as it:
                        uses = Uses(act, layer * (K * NIT) + k * NIT + it)
                        for u in range(U):
                            uses.wait(clamp_done, u)
                            act.activation(ex[:, u % 2, :], xc[:, u % 2, :], ACT.Exp).then_inc(exp_done[u % S], 1)
                            uses.wait(exp_done, u)
                            act.activation(lg[:, u % 2, :], ex[:, u % 2, :], ACT.Ln, bias=half[:, :], scale=0.5
                                           ).then_inc(log_done[u % S], 1)
                for c in range(NCH):
                    act.wait_ge(n_clamp, layer * NCH + c + 1)
                    act.activation(ex[:, c % 2, :], xc[:, c % 2, :], ACT.Exp).then_inc(n_exp, 1)
                    act.wait_ge(n_exp, layer * NCH + c + 1)
                    act.activation(lg[:, c % 2, :], ex[:, c % 2, :], ACT.Ln, bias=half[:, :], scale=0.5
                                   ).then_inc(n_act, 1)

            def layer_norm(r):
                for c in range(NCH + 1):
                    if c < NCH:
                        act.wait_ge(ln_dev, r * NCH + c + 1)
                        if c >= 2:
                            act.wait_ge(ln_var, r * NCH + c - 1)
                        act.activation(lg[:, c % 2, :], col(hT, c), ACT.Square).then_inc(ln_sq, 1)
                    if c >= 1:
                        d = c - 1
                        act.wait_ge(ln_var, r * NCH + d + 1)
                        if d >= 2:
                            act.wait_ge(ln_done, r * NCH + d - 1)
                        act.activation(ex[:, d % 2, :], ps_w[d % 2][:, :], ACT.Sqrt, bias=eps_col[:, :]
                                       ).then_inc(ln_std, 1)

            layer_norm(0)
            with act.Fori(0, L1) as g:
                project(g + L0)
                act.wait_ge(gin_w_in, g * 16 + 16)
                for c in range(NCH):
                    act.wait_ge(n_prod1, (g + L0) * NCH + c + 1)
                    if c >= 2:
                        act.wait_ge(n_prod2, (g + L0) * NCH + c - 1)
                    act.activation(hid[:, c % 2, :], ps_h[c % 2][:, :], ACT.Relu,
                                   bias=gin_w[:, GW_B1:GW_B1 + 1]).then_inc(n_act, 1)
            layer_norm(1)
            for c in range(NCH):
                done = (L0 + L1) * NCH + c
                act.wait_ge(proj_done, done + 1)
                act.copy(stage[:, c, :], ps_t[c % 2][:, :]).then_inc(proj_copied, 1)
                act.wait_ge(proj_copied, done + 3)
                full = min((N - c * CH) // P, CH // P)
                act.dma_start(out_d[c * CH:c * CH + full * P, :].rearrange("(j p) f -> p j f", p=P),
                              stage[:, c, 0:full * F].rearrange("p (j f) -> p j f", f=F)).then_inc(out_done, 16)
                rest = min(N - c * CH, CH) - full * P
                if rest:
                    act.dma_start(out_d[c * CH + full * P:N, :], stage[0:rest, c, full * F:(full + 1) * F]
                                  ).then_inc(out_done, 16)
            act.wait_ge(out_done, 16 * (NCH + (1 if N % P else 0)))

        @block.vector
        def _(dve):
            for s in clamp_done + ssp_done + msg_done + hot_done + add_done:
                dve.sem_inc(s, 1)
            dve.wait_ge(consts_in, 16 * 6)
            dst_f = rel
            dve.tensor_copy(dst_f[:, :], dst_i[:, :]).then_inc(pre, 1)
            dve.wait_ge(pre, 1)
            grouped = dst_f[:, :].rearrange("p (g t) -> p g t", t=TPG)
            dve.tensor_reduce(base_f[:, :], grouped, AX.X, ALU.min)
            dve.tensor_reduce(ends[:, 1, :], grouped, AX.X, ALU.max).then_inc(pre, 1)
            dve.wait_ge(pre, 2)
            dve.tensor_scalar(ends[:, 0, :], base_f[:, :], -1.0, None, ALU.mult).then_inc(pre, 1)
            dve.tensor_scalar(cut[:, :], len_raw[:, :], 0.0, CUTOFF, ALU.max, ALU.min).then_inc(pre, 1)
            dve.tensor_scalar(len_mask[:, :], len_raw[:, :], 0.0, None, ALU.is_ge).then_inc(pre, 1)
            dve.wait_ge(pre, 5)
            dve.scalar_tensor_tensor(out=len_raw[:, :], in0=len_raw[:, :], scalar=CUTOFF, in1=len_mask[:, :],
                                     op0=ALU.is_le, op1=ALU.mult).then_inc(pre, 1)
            dve.wait_ge(cosine_done, 1)
            dve.tensor_scalar(cut[:, :], cut[:, :], 1.0, 0.5, ALU.add, ALU.mult).then_inc(pre, 1)
            dve.wait_ge(pre, 7)
            dve.tensor_tensor(cut[:, :], cut[:, :], len_raw[:, :], ALU.mult).then_inc(pre, 1)
            dve.wait_ge(ends_reduced, 1)
            dve.tensor_scalar(base_f[:, :], ends_all[:, 0, :], -1.0, None, ALU.mult).then_inc(pre, 1)
            dve.tensor_tensor(span[:, :], ends_all[:, 0, :], ends_all[:, 1, :], ALU.add).then_inc(pre, 1)
            dve.wait_ge(pre, 10)
            dve.tensor_copy(base_i[:, :], base_f[:, :]).then_inc(pre, 1)
            dve.tensor_tensor(grouped, grouped, base_f[:, :].unsqueeze(2).broadcast_to([P, NG, TPG]),
                              ALU.subtract).then_inc(pre, 1)
            dve.tensor_reduce(span_max[:, :], span[:, :], AX.X, ALU.max).then_inc(pre, 1)
            dve.wait_ge(pre, 13)
            dve.tensor_copy(span_i[:, :], span_max[:, :]).then_inc(pre, 1)
            dve.wait_ge(pre, 14)
            dve.tensor_scalar(span_s[:, :], span_i[:, :], WIN.bit_length() - 1, None, ALU.arith_shift_right
                              ).then_inc(pre, 1)
            dve.wait_ge(pre, 15)
            dve.tensor_scalar(passes[:, :], span_s[:, :], 1.0, None, ALU.add).then_inc(pre, 1)
            dve.memset(aggT[:, :], 0.0).then_inc(agg_clear, 1)
            dve.wait_ge(pre, 16)
            dve.wait_ge(agg_clear, 1)
            dve.sem_inc(h_done, NCH)
            dve.sem_inc(ready, 1)
            K = load_passes(dve)

            def one_hot(u, factor):
                for t in range(TPG):
                    j = u * TPG + t
                    if factor:
                        op = dve.tensor_scalar(onehot[:, u % 3, t, :], win_now[:, :], rel_now[:, j:j + 1],
                                               cut_now[:, j:j + 1], ALU.is_equal, ALU.mult)
                    else:
                        op = dve.tensor_scalar(onehot[:, u % 3, t, :], win_now[:, :], rel_now[:, j:j + 1],
                                               None, ALU.is_equal)
                op.then_inc(hot_done[u % S], 1)

            def add_window(uses, u, it, k):
                start = dve.value_load(base_i[0:1, bass.ds(it * U + u, 1)], min_val=0, max_val=N)
                window = aggT[:, bass.ds(start + k * WIN, WIN)]
                uses.wait(agg_done, u)
                uses.wait(add_done, u - 1)
                dve.tensor_tensor(window, window, ps_a[u % 2][:, 0:WIN], ALU.add).then_inc(add_done[u % S], 1)

            def iteration_slices(it, n):
                dve.tensor_copy(rel_now[:, :], rel[:, bass.ds(it * (U * TPG), U * TPG)]).then_inc(slices_set, 1)
                dve.tensor_copy(cut_now[:, :], cut[:, bass.ds(it * (U * TPG), U * TPG)]).then_inc(slices_set, 1)
                dve.wait_ge(slices_set, n * 2 + 2)

            with dve.Fori(0, L0) as layer:
                dve.wait_ge(edge_w_in, layer * 32 + 32)
                dve.tensor_scalar(b1_ln2[:, :], edge_w[:, EW_B1:EW_B1 + 1], -LN2, None, ALU.add).then_inc(b1_set, 1)
                for r in range(3):
                    rest = b2_row[:, :] if r == 0 else b2_rest[:, r - 1, :]
                    dve.tensor_copy(b2_flat[:, r, :], rest).then_inc(b2_split, 1)
                    if r < 2:
                        dve.wait_ge(b2_split, layer * 5 + 2 * r + 1)
                        dve.tensor_tensor(b2_rest[:, r, :], rest, b2_flat[:, r, :], ALU.subtract).then_inc(b2_split, 1)
                        dve.wait_ge(b2_split, layer * 5 + 2 * r + 2)
                with dve.Fori(0, K) as k:
                    dve.wait_ge(b1_set, layer + 1)
                    dve.wait_ge(agg_clear, layer + 1)
                    dve.tensor_copy(win_now[:, :], iota[:, bass.ds(k * WIN, WIN)]).then_inc(win_set, 1)
                    with dve.Fori(0, NIT) as it:
                        n = dve.snap(layer * (K * NIT) + k * NIT + it)
                        dve.wait_ge(win_set, layer * K + k + 1)
                        uses = Uses(dve, n)
                        iteration_slices(it, n)
                        for i in range(U + 5):
                            if i < U:
                                uses.wait(mm1_done, i)
                                dve.tensor_scalar(xc[:, i % 2, :], ps_h[i % 2][:, :], edge_w[:, EW_B1:EW_B1 + 1],
                                                  XCLAMP, ALU.add, ALU.min).then_inc(clamp_done[i % S], 1)
                            u = i - 1
                            if 0 <= u < U:
                                uses.wait(log_done, u)
                                dve.scalar_tensor_tensor(out=hid[:, u % 3, :], in0=ps_h[u % 2][:, :],
                                                         scalar=b1_ln2[:, :], in1=lg[:, u % 2, :],
                                                         op0=ALU.add, op1=ALU.max).then_inc(ssp_done[u % S], 1)
                            u = i - 3
                            if 0 <= u < U:
                                one_hot(u, True)
                                uses.wait(mm2_done, u)
                                uses.wait_dma(rows_in, u, TPG)
                                dve.tensor_tensor(msg[:, u % 3, :], ps_w[u % 2][:, :], rows[:, u % S, :], ALU.mult
                                                  ).then_inc(msg_done[u % S], 1)
                            if i >= 5:
                                add_window(uses, i - 5, it, k)
                dve.wait_ge(node_w_in, layer * 16 + 16)
                dve.tensor_scalar(cb2_ln2[:, :], node_w[:, NW_CB2:NW_CB2 + 1], -LN2, None, ALU.add
                                  ).then_inc(cb2_set, 1)
                dve.wait_ge(cb2_set, layer + 1)
                for c in range(NCH + 2):
                    if c < NCH:
                        dve.wait_ge(n_prod1, layer * NCH + c + 1)
                        dve.tensor_scalar(xc[:, c % 2, :], ps_h[c % 2][:, :], node_w[:, NW_CB2:NW_CB2 + 1],
                                          XCLAMP, ALU.add, ALU.min).then_inc(n_clamp, 1)
                    if 1 <= c <= NCH:
                        d = c - 1
                        dve.wait_ge(n_act, layer * NCH + d + 1)
                        dve.scalar_tensor_tensor(out=hid[:, d % 2, :], in0=ps_h[d % 2][:, :], scalar=cb2_ln2[:, :],
                                                 in1=lg[:, d % 2, :], op0=ALU.add, op1=ALU.max).then_inc(n_ssp, 1)
                    if c >= 2:
                        d = c - 2
                        dve.wait_ge(n_prod2, layer * NCH + d + 1)
                        dve.scalar_tensor_tensor(out=col(hT, d), in0=ps_w[d % 2][:, :],
                                                 scalar=node_w[:, NW_LB:NW_LB + 1], in1=col(hT, d),
                                                 op0=ALU.add, op1=ALU.add).then_inc(h_done, 1)
                dve.wait_ge(h_done, layer * NCH + 2 * NCH)
                dve.sem_inc(node_w_free, 1)
                dve.memset(aggT[:, :], 0.0).then_inc(agg_clear, 1)

            def layer_norm(r, keep):
                for c in range(NCH):
                    dve.tensor_tensor(col(hT, c), col(hT, c), col(xT, c), ALU.add).then_inc(ln_sum, 1)
                for c in range(NCH + 2):
                    if c < NCH:
                        dve.wait_ge(ln_mean, r * NCH + c + 1)
                        dve.tensor_tensor(col(hT, c), col(hT, c), ps_h[c % 2][:, :], ALU.subtract
                                          ).then_inc(ln_dev, 1)
                    if c >= 2:
                        d = c - 2
                        dve.wait_ge(ln_std, r * NCH + d + 1)
                        dve.reciprocal(ex[:, d % 2, :], ex[:, d % 2, :]).then_inc(ln_inv, 1)
                        dve.wait_ge(ln_inv, r * NCH + d + 1)
                        dve.tensor_tensor(col(hT, d), col(hT, d), ex[:, d % 2, :], ALU.mult).then_inc(ln_done, 1)
                        if keep:
                            dve.wait_ge(ln_done, r * NCH + d + 1)
                            dve.tensor_copy(col(xT, d), col(hT, d)).then_inc(ln_keep, 1)

            layer_norm(0, True)
            dve.wait_ge(ln_keep, NCH)
            with dve.Fori(0, L1) as g:
                dve.wait_ge(gin_w_in, g * 16 + 16)
                dve.tensor_scalar(eps1[:, :], gin_w[:, GW_EPS:GW_EPS + 1], 1.0, None, ALU.add).then_inc(eps1_set, 1)
                with dve.Fori(0, K) as k:
                    dve.wait_ge(eps1_set, g + 1)
                    dve.wait_ge(agg_clear, g + (L0 + 1))
                    dve.tensor_copy(win_now[:, :], iota[:, bass.ds(k * WIN, WIN)]).then_inc(win_set, 1)
                    with dve.Fori(0, NIT) as it:
                        n = dve.snap((g + L0) * (K * NIT) + k * NIT + it)
                        dve.wait_ge(win_set, (g + L0) * K + k + 1)
                        uses = Uses(dve, n)
                        iteration_slices(it, n)
                        for i in range(U + 1):
                            if i < U:
                                one_hot(i, False)
                            if i >= 1:
                                add_window(uses, i - 1, it, k)
                                dve.sem_inc(msg_done[(i - 1) % S], 1)
                for c in range(NCH + 2):
                    if c < NCH:
                        if c >= 2:
                            dve.wait_ge(n_prod1, (g + L0) * NCH + c - 1)
                        dve.scalar_tensor_tensor(out=xc[:, c % 2, :], in0=col(hT, c), scalar=eps1[:, :],
                                                 in1=col(aggT, c), op0=ALU.mult, op1=ALU.add).then_inc(z_done, 1)
                    if c >= 2:
                        d = c - 2
                        dve.wait_ge(n_prod2, (g + L0) * NCH + d + 1)
                        dve.tensor_scalar(col(hT, d), ps_w[d % 2][:, :], gin_w[:, GW_B2:GW_B2 + 1], None, ALU.add
                                          ).then_inc(h_done, 1)
                dve.wait_ge(h_done, (g + L0 + 2) * NCH)
                dve.sem_inc(gin_w_free, 1)
                dve.memset(aggT[:, :], 0.0).then_inc(agg_clear, 1)
            layer_norm(1, False)


def kernel(x, src, dst, edge_attr_100, edge_weight, L0_gnn_mlp_w1, L0_gnn_mlp_b1, L0_gnn_mlp_w2, L0_gnn_mlp_b2,
           L0_gnn_conv_w1, L0_gnn_conv_w2, L0_gnn_conv_b2, L0_gnn_lin_w, L0_gnn_lin_b,
           L1_gnn_W1, L1_gnn_b1, L1_gnn_W2, L1_gnn_b2, L1_gnn_eps):
    import numpy as np
    import concourse.bacc as bacc
    from concourse.bass_utils import run_bass_kernel_spmd

    def arr(a):
        return np.asarray(a)

    def padded(a, n, value=0):
        return np.concatenate([a, np.full((n - a.shape[0],) + a.shape[1:], value, a.dtype)])

    def by_column(a):
        return np.ascontiguousarray(a.reshape(NG * TPG, P).T)

    xT = np.ascontiguousarray(padded(arr(x), NP).T)
    src_g = np.ascontiguousarray(padded(arr(src), EP).reshape(NG, TPG, P).transpose(0, 2, 1))
    dst_c = by_column(padded(arr(dst), EP, N))
    ew_c = by_column(padded(arr(edge_weight), EP))
    attr = np.ascontiguousarray(padded(arr(edge_attr_100), EP).reshape(NG, GE, G).transpose(0, 2, 1))
    w1 = np.zeros((L0, P, F), np.float32)
    w1[:, :G] = arr(L0_gnn_mlp_w1)
    edge_w = np.concatenate([w1, arr(L0_gnn_mlp_w2), arr(L0_gnn_conv_w1), arr(L0_gnn_mlp_b1)[:, :, None]], axis=2)
    b2_row = np.ascontiguousarray(np.tile(arr(L0_gnn_mlp_b2), (1, TPG))[:, None, :])
    node_w = np.concatenate([arr(L0_gnn_conv_w2), arr(L0_gnn_lin_w), arr(L0_gnn_conv_b2)[:, :, None],
                             arr(L0_gnn_lin_b)[:, :, None]], axis=2)
    eps = np.ascontiguousarray(np.broadcast_to(arr(L1_gnn_eps)[:, None, None], (L1, P, 1)))
    gin_w = np.concatenate([arr(L1_gnn_W1), arr(L1_gnn_W2), arr(L1_gnn_b1)[:, :, None],
                            arr(L1_gnn_b2)[:, :, None], eps], axis=2)
    ident = np.eye(P, dtype=np.float32)
    iota = np.ascontiguousarray(np.broadcast_to(np.arange(KMAX * WIN, dtype=np.float32), (P, KMAX * WIN)))

    nc = bacc.Bacc("TRN2", target_bir_lowering=False, num_devices=1)
    arrays, args = {}, []
    for name, a in (("xT", xT), ("src", src_g), ("dst", dst_c), ("edge_len", ew_c), ("attr", attr),
                    ("edge_w", edge_w), ("b2_row", b2_row), ("node_w", node_w), ("gin_w", gin_w),
                    ("ident", ident), ("iota", iota)):
        arrays[f"in_{name}"] = a
        args.append(nc.dram_tensor(f"in_{name}", a.shape, mybir.dt.from_np(a.dtype), kind="ExternalInput").ap())
    out = nc.dram_tensor("out", (N, F), mybir.dt.float32, kind="ExternalOutput").ap()
    gnn_program(nc, *args, out)
    return run_bass_kernel_spmd(nc, [arrays], core_ids=[0]).results[0]["out"]
```

```python
import concourse.bass as bass
from concourse import mybir
from contextlib import ExitStack
import math

P = 128
N = 2500
E = 82500
F = 128
G = 100
L0 = 6
L1 = 3
TPG = 4
GE = TPG * P
S = 6
U = 18
Q = U // S
NG = -(-E // GE)
NIT = NG // U
assert NG % U == 0 and U % S == 0
EP = NG * GE
LAST_TILES = -(-(E - (NG - 1) * GE) // P)
WIN = 32
KMAX = N // WIN + 1
CH = 512
NCH = -(-N // CH)
NP = NCH * CH
START_MAX = N
NCOL = N + WIN
NB = NP // P
HB = 2
BG = NG // (L0 * NIT)
BT = BG * TPG
EARLY_AT = [(c + 1) * CH * NIT // N + 1 for c in range(NCH - 1)]
assert len(set(EARLY_AT)) == NCH - 1 and EARLY_AT[-1] < NIT
assert S % HB == 0 and U % HB == 0
assert BG * L0 * NIT == NG and BG == Q
COUNT_MAX = 255
CUTOFF = 10.0
LN2 = math.log(2.0)
XCLAMP = 40.0
LN_EPS = 1e-5

EW_W1, EW_W2, EW_B1, EW_N = 0, F, 2 * F, 2 * F + 1
NW_CW2, NW_LIN, NW_NEXT, NW_CB2, NW_LB, NW_N = 0, F, 2 * F, 3 * F, 3 * F + 1, 3 * F + 2
GW_W1, GW_W2, GW_B1, GW_B2, GW_EPS, GW_N = 0, F, 2 * F, 2 * F + 1, 2 * F + 2, 2 * F + 3
COUNT_STEP = {4 + q + q // TPG: q for q in range(BT)}


def gnn_program(nc, xT_d, src_d, srcc_d, dst_d, plan_d, ew_d, attr_d, edge_w_d, b2_d, first_w_d, node_w_d, gin_w_d,
                ident_d, iota_d, out_d):
    f32, i32, bf16, i16 = mybir.dt.float32, mybir.dt.int32, mybir.dt.bfloat16, mybir.dt.int16
    ACT, ALU, AX = mybir.ActivationFunctionType, mybir.AluOpType, mybir.AxisListType
    RMAX = bass.bass_isa.ReduceOp.max
    table_d = [nc.dram_tensor(f"node_table{i}", [NP, F], f32, kind="Internal").ap() for i in range(2)]

    with ExitStack() as ctx:
        def sb(name, shape, dt=f32):
            return ctx.enter_context(nc.sbuf_tensor(name, shape, dt))

        def psum(name, n):
            return [ctx.enter_context(nc.psum_tensor(f"{name}{i}", [P, 512], f32)) for i in range(n)]

        def sem(name):
            return ctx.enter_context(nc.semaphore(name))

        def slot_sems(name, n=S):
            return [sem(f"{name}{i}") for i in range(n)]

        hT = sb("hT", [P, NP])
        aggT = sb("aggT", [P, NP])
        ident = sb("ident", [P, P])
        mean_mat = sb("mean_mat", [P, P])
        ones3 = sb("ones3", [3, P], bf16)
        iota = sb("iota", [P, NP], i16)
        half_col = sb("half_col", [P, 1])
        half_pi = sb("half_pi", [P, 1])
        eps_col = sb("eps_col", [P, 1])

        plan = sb("plan", [P, NG + NIT])
        early_now = sb("early_now", [P, NIT], i32)
        slack = sb("slack", [P, 1])
        sorted_dst = sb("sorted_dst", [P, 1])
        edge_w = sb("edge_w", [P, EW_N])
        b1_ln2 = sb("b1_ln2", [P, 1])
        b2_row = sb("b2_row", [1, F])
        b2_rest = sb("b2_rest", [1, 2, F])
        b2_flat = sb("b2_flat", [1, 3, F], bf16)
        b2_parts = sb("b2_parts", [3, GE], bf16)
        node_w = sb("node_w", [P, NW_N])
        cb2_ln2 = sb("cb2_ln2", [P, 1])
        gin_w = node_w[:, 0:GW_N]
        eps1 = sb("eps1", [P, 1])
        rel = sb("rel", [P, NG * TPG])
        cut = sb("cut", [P, NG * TPG])
        base_f = sb("base_f", [P, NG])
        base_i = sb("base_i", [P, NG], i32)
        span_max = sb("span_max", [P, 1])
        span_i = sb("span_i", [P, 1], i32)
        span_s = sb("span_s", [P, 1], i32)
        passes = sb("passes", [P, 1], i32)
        counts = sb("counts", [P, NB + 1, NCOL], bf16)
        src_f = sb("src_f", [P, NG * TPG])
        scratch = counts[:, :, :].rearrange("p b n -> p (b n)").bitcast(f32)
        dst_i, src_i, len_raw, len_mask = (scratch[:, i * NG * TPG:(i + 1) * NG * TPG] for i in range(4))
        dst_i, src_i = dst_i.bitcast(i32), src_i.bitcast(i32)
        ends, ends_all, span = (scratch[:, (4 * TPG + 2 * i) * NG:(4 * TPG + min(2 * i + 2, 5)) * NG] for i in range(3))
        TABLES, ALL = (4 * TPG + 5) * NG, (NB + 1) * NCOL // 2
        CLEAR_ACT = TABLES + 2 * NP
        CLEAR_WAITING = CLEAR_ACT + 2400
        CLEAR_DVE = CLEAR_ACT + 7000
        CLEAR_POOL = CLEAR_DVE + 4800
        ends, ends_all = (t.rearrange("p (a g) -> p a g", a=2) for t in (ends, ends_all))
        src_hot = sb("src_hot", [P, 2, NP], bf16)
        dst_hot = sb("dst_hot", [P, 2, TPG, WIN], bf16)
        ones_mat = sb("ones_mat", [P, P], bf16)
        rel_count = sb("rel_count", [P, BT])
        src_count = sb("src_count", [P, BT])
        most_edges = sb("most_edges", [P, 1])
        most_edges_i = sb("most_edges_i", [P, 1], i32)
        attr_buf = sb("attr_buf", [P, S, GE])
        attr = attr_buf[0:G]
        xT = attr_buf[:, 0:NCH, :].rearrange("p c n -> p (c n)")
        idx = sb("idx", [P, S, TPG], i32)
        rows = sb("rows", [P, S, GE])
        stage = rows[:, 0:NCH, :]
        rel_now = sb("rel_now", [P, U * TPG])
        cut_now = sb("cut_now", [P, U * TPG])
        win_now = sb("win_now", [P, WIN])
        xc = sb("xc", [P, 2, GE])
        first_w = xc[:, 1, 0:F]
        ex = sb("ex", [P, 2, GE])
        stage_one, step_one = ex[:, 0, :], ex[:, 1, :]
        lg = sb("lg", [P, 2, GE])
        hid = sb("hid", [P, 3, GE])
        msg = sb("msg", [P, 3, GE])
        onehot = sb("onehot", [P, 2, HB * TPG, WIN])
        msg_flat = msg[:, :, :].rearrange("p b n -> p (b n)").bitcast(bf16)
        hi, mid, lo = parts = [src_hot[:, 0, :], src_hot[:, 1, :], msg_flat[:, 0:NP]]

        ps_h, ps_w, ps_a = (psum(name, 2) for name in ("ps_h", "ps_w", "ps_a"))
        ps_pair = ctx.enter_context(nc.psum_tensor("ps_pair", [P, 1024], f32))
        ps_t = [ps_pair[:, 0:512], ps_pair[:, 512:1024]]
        ps_c = ps_pair[:, 0:(NB + 1) * WIN]

        dst_in, first_in, plan_in, consts_in, consts_set = (sem(s) for s in
            ("dst_in", "first_in", "plan_in", "consts_in", "consts_set"))
        pre = sem("pre")
        ends_reduced, cosine_done, ready = sem("ends_reduced"), sem("cosine_done"), sem("ready")
        edge_w_in, node_w_in, gin_w_in = sem("edge_w_in"), sem("node_w_in"), sem("gin_w_in")
        b2_split, b2_in = sem("b2_split"), sem("b2_in")
        gin_w_free = sem("gin_w_free")
        b1_set, cb2_set, eps1_set = sem("b1_set"), sem("cb2_set"), sem("eps1_set")
        table_in = sem("table_in")
        early_set, act_cleared, pool_cleared, dve_cleared = (sem(s) for s in
            ("early_set", "act_cleared", "pool_cleared", "dve_cleared"))
        attr_in, idx_in, rows_in = slot_sems("attr_in"), slot_sems("idx_in"), slot_sems("rows_in")
        mm1_done, clamp_done, log_done, ssp_done = (slot_sems(s) for s in ("mm1_", "clamp_", "log_", "ssp_"))
        mm2_done, msg_done, hot_done, agg_done, add_done = (slot_sems(s) for s in
                                                            ("mm2_", "msg_", "hot_", "agg_", "add_"))
        equal_done = slot_sems("equal_")
        exp_done = slot_sems("exp_")
        slices_set, win_set, count_slices = sem("slices_set"), sem("win_set"), sem("count_slices")
        tile_hot, tile_counted = slot_sems("tile_hot", TPG), slot_sems("tile_counted", TPG)
        count_added = sem("count_added")
        counts_ready = sem("counts_ready")
        hi_done, mid_done, lo_done, agg_sum, agg_in = (sem(s) for s in
            ("hi_done", "mid_done", "lo_done", "agg_sum", "agg_in"))
        proj_done, proj_copied = sem("proj_done"), sem("proj_copied")
        n_prod1, n_clamp, n_exp, n_act, n_ssp, n_prod2 = (sem(s) for s in
            ("n_prod1", "n_clamp", "n_exp", "n_act", "n_ssp", "n_prod2"))
        turned, staged, rest_done = sem("turned"), sem("staged"), sem("rest_done")
        out_prod, out_copied = sem("out_prod"), sem("out_copied")
        half_step = sem("half_step")
        HALF_PROD1, HALF_CLAMP, HALF_EXP, HALF_ACT, HALF_SSP, HALF_PROD2, HALF_H, HALF_PROJ, HALF_COPIED = range(1, 10)
        x_in, h_kept = sem("x_in"), sem("h_kept")
        h_done, agg_clear, z_done = sem("h_done"), sem("agg_clear"), sem("z_done")
        ln_sum, ln_mean, ln_dev, ln_sq, ln_var, ln_newton, ln_log, ln_inv, ln_done, ln_keep = (sem(s) for s in
            ("ln_sum", "ln_mean", "ln_dev", "ln_sq", "ln_var", "ln_newton", "ln_log", "ln_inv", "ln_done", "ln_keep"))
        out_done = sem("out_done")
        gate = sem("gate")

        table_rows = [t.rearrange("(c j p) f -> c p j f", j=CH // P, p=P) for t in table_d]

        def load_passes(eng):
            eng.wait_ge(ready, 1)
            return eng.value_load(passes[0:1, 0:1], min_val=1, max_val=KMAX)

        class Uses:

            def __init__(self, eng, n):
                self.eng, self.n, self.regs = eng, n, {}

            def value(self, u, scale=1, prime=1):
                key = (u // S + prime, scale)
                if key not in self.regs:
                    self.regs[key] = self.eng.snap((self.n * Q + (key[0] + 1)) * scale)
                return self.regs[key]

            def wait(self, sems, u):
                self.eng.wait_ge(sems[u % S], self.value(u))

            def wait_count(self, sem, j):
                self.eng.wait_ge(sem, self.value(j * S))

            def wait_dma(self, sems, u, dmas=1):
                self.eng.wait_ge(sems[u % S], self.value(u, 16 * dmas, 0))

        def wait_rows(eng, done, it, u):
            skipped = 16 * (TPG - LAST_TILES) if u % S == (U - 1) % S else 0
            value = done * (NIT * Q * TPG * 16 - skipped) + it * (Q * TPG * 16)
            landed = (u // S + 1) * (TPG * 16)
            if u == U - 1:
                bits = (NIT - 2).bit_length()
                not_last = (it + (2 * 2 ** bits - (NIT - 1))) >> bits & 1
                value, landed = value + not_last * skipped, landed - skipped
            eng.wait_ge(rows_in[u % S], eng.snap(value + landed))

        def half_steps(layer, step_a, sem_b, before=0):
            return ((0, slice(0, CH // 2), half_step, layer * HALF_COPIED + step_a),
                    (1, slice(CH // 2, CH), sem_b, layer * NCH + NCH + before))

        def nodes_in(c):
            return min(CH, N - c * CH)

        def col(t, c):
            return t[:, c * CH:(c + 1) * CH]

        def load_early(eng, it, least=0):
            return eng.value_load(early_now[0:1, bass.ds(it, 1)], min_val=least, max_val=NCH - 1)

        def load_most_edges(eng):
            eng.wait_ge(counts_ready, 1)
            return eng.value_load(most_edges_i[0:1, 0:1], min_val=0, max_val=COUNT_MAX + 1)

        def b2_loads(eng, layer):
            eng.wait_ge(b2_split, layer * 5 + 5)
            for t in range(TPG):
                eng.dma_start(b2_parts[:, t * F:(t + 1) * F], b2_flat[0:1, :, :]).then_inc(b2_in, 16)

        block = ctx.enter_context(nc.Block())

        @block.sync
        def _(sp):
            sp.dma_start(dst_i, dst_d).then_inc(dst_in, 16)
            sp.dma_start(first_w, first_w_d).then_inc(first_in, 16)
            sp.dma_start(hT[:, :], xT_d).then_inc(first_in, 16)
            sp.dma_start(plan[:, :], plan_d).then_inc(plan_in, 16)
            for t, s in ((len_raw, ew_d), (src_i, srcc_d), (ident, ident_d), (iota, iota_d)):
                sp.dma_start(t[:, :], s).then_inc(consts_in, 16)

            def edge_weights(layer):
                sp.dma_start(edge_w[:, :], edge_w_d[bass.ds(layer, 1)].rearrange("a p t -> (a p) t")
                             ).then_inc(edge_w_in, 16)
                sp.dma_start(b2_row[:, :], b2_d[bass.ds(layer, 1)].rearrange("a p t -> (a p) t")
                             ).then_inc(edge_w_in, 16)

            sp.dma_start(node_w[:, :], node_w_d[0]).then_inc(node_w_in, 16)
            edge_weights(0)
            K = load_passes(sp)

            def edge_loads(layer, with_attr):
                with sp.Fori(0, K) as k:
                    with sp.Fori(0, NIT) as it:
                        uses = Uses(sp, layer * (K * NIT) + k * NIT + it)
                        for u in range(U):
                            g = it * U + u
                            uses.wait(msg_done, u - S)
                            sp.dma_start(idx[:, u % S, :], src_d[bass.ds(g, 1)].rearrange("a p t -> (a p) t")
                                         ).then_inc(idx_in[u % S], 16)
                            if with_attr:
                                uses.wait(mm1_done, u - S)
                                sp.dma_start(attr[:, u % S, :], attr_d[bass.ds(g, 1)].rearrange("a p t -> (a p) t")
                                             ).then_inc(attr_in[u % S], 16)

            with sp.Fori(0, L0) as layer:
                edge_loads(layer, True)
                with sp.If(layer < L0 - 1):
                    sp.wait_ge(add_done[(U - 1) % S], (layer + 1) * (K * (NIT * Q)) + 1)
                    edge_weights(layer + 1)
            sp.wait_ge(add_done[(U - 1) % S], L0 * (K * (NIT * Q)) + 1)
            sp.dma_start(xT, xT_d).then_inc(x_in, 16)
            sp.wait_ge(node_w_in, 16 * (L0 + 1))
            sp.wait_ge(proj_done, (L0 + 1) * NCH)
            most = load_most_edges(sp)
            with sp.Fori(0, L1) as g:
                sp.wait_ge(gin_w_free, g + 1)
                sp.dma_start(gin_w[:, :], gin_w_d[bass.ds(g, 1)].rearrange("a p t -> (a p) t")
                             ).then_inc(gin_w_in, 16)
                with sp.If(most > COUNT_MAX):
                    edge_loads(L0 + g, False)

        @block.gpsimd
        def _(pool):
            pool.memset(half_pi[:, :], math.pi / 2).then_inc(consts_set, 1)
            pool.memset(half_col[:, :], 0.5).then_inc(consts_set, 1)
            pool.memset(ones3[:, :], 1.0).then_inc(consts_set, 1)
            pool.memset(ones_mat[:, :], 1.0).then_inc(consts_set, 1)
            pool.memset(mean_mat[:, :], 1.0 / F).then_inc(consts_set, 1)
            pool.memset(eps_col[:, :], LN_EPS).then_inc(consts_set, 1)
            pool.memset(scratch[:, CLEAR_DVE:CLEAR_POOL], 0.0).then_inc(pool_cleared, 1)
            pool.wait_ge(pre, 3)
            pool.partition_all_reduce(ends_all[:, :, :].rearrange("p a g -> p (a g)"),
                                      ends[:, :, :].rearrange("p a g -> p (a g)"), P, RMAX).then_inc(ends_reduced, 1)
            pool.memset(scratch[:, CLEAR_POOL:ALL], 0.0).then_inc(pool_cleared, 1)
            K = load_passes(pool)

            def gather(layer, tables, half):
                pool.wait_ge(table_in, tables * (16 * NCH))
                pool.sem_inc(gate, 1)
                with pool.Fori(0, K) as k:
                    with pool.Fori(0, NIT) as it:
                        uses = Uses(pool, layer * (K * NIT) + k * NIT + it)
                        for u in range(U):
                            uses.wait_dma(idx_in, u)
                            uses.wait(msg_done, u - S)
                            pool.sem_inc(gate, 1)

                            def gather_tiles(tiles):
                                for t in tiles:
                                    pool.indirect_dma_start(
                                        out=rows[:, u % S, t * F:(t + 1) * F], out_offset=None, in_=table_d[half][:, :],
                                        in_offset=bass.IndirectOffsetOnAxis(ap=idx[:, u % S, t:t + 1], axis=0),
                                    ).then_inc(rows_in[u % S], 16)

                            if u < U - 1:
                                gather_tiles(range(TPG))
                            else:
                                gather_tiles(range(LAST_TILES))
                                with pool.If(it < NIT - 1):
                                    gather_tiles(range(LAST_TILES, TPG))

            with pool.Fori(0, L0 // 2) as pair:
                for half in range(2):
                    layer = pool.snap(pair * 2 + half)
                    gather(layer, layer + 1, half)
            most = load_most_edges(pool)
            with pool.If(most > COUNT_MAX):
                with pool.Fori(L0, L0 + L1) as layer:
                    gather(layer, layer + 2, 0)

        @block.tensor
        def _(pe):
            for s in mm1_done + mm2_done + agg_done + tile_counted:
                pe.sem_inc(s, 1)

            def project(c, m, copied):
                pe.wait_ge(proj_copied, copied)
                for j in range(CH // P):
                    mm = pe.matmul(ps_t[c % 2][:, j * P:(j + 1) * P], hT[:, c * CH + j * P:c * CH + (j + 1) * P],
                                   m, start=True, stop=True)
                mm.then_inc(proj_done, 1)

            pe.wait_ge(first_in, 32)
            for c in range(NCH):
                project(c, first_w, c + 1)
            pe.wait_ge(consts_in, 16 * 4)
            pe.wait_ge(consts_set, 6)
            K = load_passes(pe)

            def aggregate(uses, u, source):
                uses.wait(hot_done, u - u % HB)
                uses.wait(add_done, u - 2)
                for t in range(TPG):
                    mm = pe.matmul(ps_a[u % 2][:, 0:WIN], source[:, t * F:(t + 1) * F], onehot[:, u // HB % 2, u % HB * TPG + t, :],
                                   start=(t == 0), stop=(t == TPG - 1))
                mm.then_inc(agg_done[u % S], 1)

            def count_tile(uses, q):
                j, t = q // TPG, q % TPG
                uses.wait_count(tile_hot[t], j)
                if t == 0:
                    uses.wait_count(count_added, j - 1)
                for b in range(NB + 1):
                    src_side = src_hot[:, q % 2, b * P:(b + 1) * P] if b < NB else ones_mat[:, :]
                    mm = pe.matmul(ps_c[:, b * WIN:(b + 1) * WIN], src_side, dst_hot[:, j % 2, t, :],
                                   start=(t == 0 and b % (512 // WIN) == 0), stop=(t == TPG - 1),
                                   skip_group_check=True)
                mm.then_inc(tile_counted[t], 1)

            def chunk_prod1(start, done):
                pe.wait_ge(proj_copied, done + (NCH + 1))
                pe.matmul(ps_t[0], node_w[:, NW_CW2:NW_CW2 + F], aggT[:, bass.ds(start, CH)],
                          start=True, stop=True).then_inc(n_prod1, 1)

            def chunk_prod2(done):
                pe.wait_ge(n_ssp, done)
                pe.matmul(ps_t[1], node_w[:, NW_LIN:NW_LIN + F], step_one, start=True, stop=True
                          ).then_inc(n_prod2, 1)

            def chunk_project(done):
                pe.wait_ge(h_done, done)
                for j in range(CH // P):
                    mm = pe.matmul(ps_t[0][:, j * P:(j + 1) * P], step_one[:, j * P:(j + 1) * P],
                                   node_w[:, NW_NEXT:NW_NEXT + F], start=True, stop=True)
                mm.then_inc(proj_done, 1)

            pe.wait_ge(early_set, 1)
            with pe.Fori(0, L0) as layer:
                with pe.Fori(0, K) as k:
                    with pe.Fori(0, NIT) as it:
                        uses = Uses(pe, layer * (K * NIT) + k * NIT + it)
                        for i in range(U + 4):
                            if i == 0:
                                pe.wait_ge(edge_w_in, layer * 32 + 32)
                                pe.wait_ge(b2_in, layer * (16 * TPG) + 16 * TPG)
                            if i < U:
                                uses.wait_dma(attr_in, i)
                                uses.wait(ssp_done, i - 2)
                                pe.matmul(ps_h[i % 2][:, :], edge_w[0:G, EW_W1:EW_W1 + F], attr[:, i % S, :],
                                          start=True, stop=True).then_inc(mm1_done[i % S], 1)
                            u = i - 2
                            if 0 <= u < U:
                                uses.wait(ssp_done, u)
                                uses.wait(msg_done, u - 2)
                                pe.matmul(ps_w[u % 2][:, :], ones3[:, :], b2_parts[:, :], start=True, stop=False)
                                for t in range(TPG):
                                    mm = pe.matmul(ps_w[u % 2][:, t * F:(t + 1) * F], hid[:, u % 3, t * P:(t + 1) * P],
                                                   edge_w[:, EW_W2:EW_W2 + F], start=False, stop=(t == TPG - 1))
                                mm.then_inc(mm2_done[u % S], 1)
                            u = i - 4
                            if u >= 0:
                                uses.wait(msg_done, u)
                                aggregate(uses, u, msg[:, u % 3, :])
                            if i == 0:
                                with pe.If(load_early(pe, it) > 0):
                                    early = load_early(pe, it, 1)
                                    pe.wait_ge(node_w_in, layer * 16 + 16)
                                    uses.wait(add_done, -1)
                                    uses.wait_count(count_added, -1)
                                    chunk_prod1(pe.snap(early * CH - CH), layer * NCH + early)
                            if i == 2:
                                with pe.If(load_early(pe, it) > 0):
                                    chunk_prod2(layer * NCH + load_early(pe, it, 1))
                            if i == 3:
                                with pe.If(load_early(pe, it) > 0):
                                    chunk_project(layer * NCH + load_early(pe, it, 1))
                            if i - 1 in COUNT_STEP:
                                count_tile(uses, COUNT_STEP[i - 1])
                with pe.If(load_early(pe, NIT - 1) > 0):
                    pe.wait_ge(node_w_in, layer * 16 + 16)
                    pe.wait_ge(add_done[(U - 1) % S], (layer + 1) * (K * (NIT * Q)) + 1)
                    for i, half, signal, _ in half_steps(layer, HALF_PROD1, n_prod1):
                        pe.matmul(ps_h[i][:, 0:CH // 2], node_w[:, NW_CW2:NW_CW2 + F], col(aggT, NCH - 1)[:, half],
                                  start=True, stop=True).then_inc(signal, 1)
                    for (i, half, ssp, value), signal in zip(half_steps(layer, HALF_SSP, n_ssp), (half_step, n_prod2)):
                        pe.wait_ge(ssp, value)
                        pe.matmul(ps_w[i][:, 0:CH // 2], node_w[:, NW_LIN:NW_LIN + F], step_one[:, half],
                                  start=True, stop=True).then_inc(signal, 1)
                    for (i, half, h, value), signal in zip(half_steps(layer, HALF_H, h_done), (half_step, proj_done)):
                        pe.wait_ge(h, value)
                        pe.wait_ge(proj_copied, layer * NCH + (2 * NCH + 1))
                        for j in range(CH // P // 2):
                            mm = pe.matmul(ps_t[i][:, j * P:(j + 1) * P], step_one[:, half][:, j * P:(j + 1) * P],
                                           node_w[:, NW_NEXT:NW_NEXT + F], start=True, stop=True)
                        mm.then_inc(signal, 1)
                with pe.Else():
                    pe.wait_ge(node_w_in, layer * 16 + 16)
                    pe.wait_ge(add_done[(U - 1) % S], (layer + 1) * (K * (NIT * Q)) + 1)
                    for c in range(NCH + 2):
                        if c < NCH:
                            if c >= 2:
                                pe.wait_ge(n_ssp, layer * NCH + c - 1)
                            pe.matmul(ps_h[c % 2][:, :], node_w[:, NW_CW2:NW_CW2 + F], col(aggT, c),
                                      start=True, stop=True).then_inc(n_prod1, 1)
                        d = c - 1
                        if 0 <= d < NCH:
                            pe.wait_ge(n_ssp, layer * NCH + d + 1)
                            if d >= 2:
                                pe.wait_ge(h_done, layer * NCH + d - 1)
                            pe.matmul(ps_w[d % 2][:, :], node_w[:, NW_LIN:NW_LIN + F], hid[:, d % 2, :],
                                      start=True, stop=True).then_inc(n_prod2, 1)
                        d = c - 2
                        if d >= 0:
                            pe.wait_ge(h_done, layer * NCH + d + 1)
                            project(d, node_w[:, NW_NEXT:NW_NEXT + F], layer * NCH + NCH + d + 1)

            def layer_norm(r):
                for c in range(NCH + 1):
                    if c < NCH:
                        pe.wait_ge(ln_sum, r * NCH + c + 1)
                        if c >= 2:
                            pe.wait_ge(ln_dev, r * NCH + c - 1)
                        pe.matmul(ps_h[c % 2][:, :], mean_mat[:, :], col(hT, c), start=True, stop=True
                                  ).then_inc(ln_mean, 1)
                    if c >= 1:
                        d = c - 1
                        pe.wait_ge(ln_sq, r * NCH + d + 1)
                        if d >= 2:
                            pe.wait_ge(ln_done, r * NCH + d - 1)
                        pe.matmul(ps_w[d % 2][:, :], mean_mat[:, :], lg[:, d % 2, :], start=True, stop=True
                                  ).then_inc(ln_var, 1)

            layer_norm(0)
            def gin_prod1(g, c):
                pe.wait_ge(z_done, g * NCH + c + 1)
                if c >= 2:
                    pe.wait_ge(n_act, (g + L0) * NCH + c - 1)
                pe.matmul(ps_h[c % 2][:, :], gin_w[:, GW_W1:GW_W1 + F], xc[:, c % 2, :],
                          start=True, stop=True).then_inc(n_prod1, 1)

            def gin_prod2(g, c):
                pe.wait_ge(n_act, (g + L0) * NCH + c + 1)
                if c >= 2:
                    pe.wait_ge(h_done, (g + L0) * NCH + c - 1)
                pe.matmul(ps_w[c % 2][:, :], gin_w[:, GW_W2:GW_W2 + F], hid[:, c % 2, :],
                          start=True, stop=True).then_inc(n_prod2, 1)

            def turn(g, c):
                if c >= 2 or not isinstance(g, int):
                    pe.wait_ge(staged, g * NCH + c - 1)
                for j in range(CH // P):
                    mm = pe.matmul(ps_a[c % 2][:, j * P:(j + 1) * P], hT[:, c * CH + j * P:c * CH + (j + 1) * P],
                                   ident[:, :], start=True, stop=True)
                mm.then_inc(turned, 1)

            def sums(g, c, r, blocks):
                for b in blocks:
                    first, last = (r, b) == (0, 0), (r, b) == (2, NB - 1)
                    if c == 0 and b % (CH // P) == 0:
                        pe.wait_ge((hi_done, mid_done, lo_done)[r], g * NCH + b // (CH // P) + 1)
                    if first:
                        pe.wait_ge(agg_in, g * NCH + c + 1)
                    mm = pe.matmul(ps_t[c % 2][:, 0:nodes_in(c)], parts[r][:, b * P:(b + 1) * P],
                                   counts[:, b, c * CH:c * CH + nodes_in(c)], start=first, stop=last)
                    if last:
                        mm.then_inc(agg_sum, 1)

            most = load_most_edges(pe)
            with pe.If(most > COUNT_MAX):
                with pe.Fori(0, L1) as g:
                    for c in range(NCH):
                        pe.wait_ge(ln_done, NCH)
                        pe.wait_ge(h_done, g * NCH + L0 * NCH)
                        project(c, ident[:, :], g * NCH + (L0 + 1) * NCH + c + 1)
                    with pe.Fori(0, K) as k:
                        with pe.Fori(0, NIT) as it:
                            uses = Uses(pe, (g + L0) * (K * NIT) + k * NIT + it)
                            for u in range(U):
                                wait_rows(pe, (g + L0) * K + k, it, u)
                                aggregate(uses, u, rows[:, u % S, :])
                    for c in range(NCH + 1):
                        if c < NCH:
                            pe.wait_ge(gin_w_in, g * 16 + 16)
                            gin_prod1(g, c)
                        if c >= 1:
                            gin_prod2(g, c - 1)
            with pe.Else():
                for c in range(NCH - 1):
                    pe.wait_ge(ln_done, c + 1)
                    turn(0, c)
                pe.wait_ge(ln_done, NCH)
                with pe.Fori(0, L1) as g:
                    early, late = range(0, NB - CH // P), range(NB - CH // P, NB)
                    sums(g, 0, 0, early)
                    pe.wait_ge(h_done, (g + L0) * NCH)
                    turn(g, NCH - 1)
                    sums(g, 0, 1, early)
                    sums(g, 0, 0, late)
                    sums(g, 0, 1, late)
                    sums(g, 0, 2, range(NB))
                    for c in range(1, NCH + 1):
                        if c < NCH:
                            sums(g, c, 0, range(NB))
                        if c == 1:
                            pe.wait_ge(gin_w_in, g * 16 + 16)
                        gin_prod1(g, c - 1)
                        if c < NCH:
                            sums(g, c, 1, range(NB))
                        gin_prod2(g, c - 1)
                        if c < NCH:
                            sums(g, c, 2, range(NB // 2))
                            pe.wait_ge(h_done, (g + L0) * NCH + c)
                            turn(g + 1, c - 1)
                            sums(g, c, 2, range(NB // 2, NB))
            layer_norm(1)
            for c in range(NCH):
                pe.wait_ge(ln_done, NCH + c + 1)
                if c >= 2:
                    pe.wait_ge(out_copied, c - 1)
                for j in range(CH // P):
                    mm = pe.matmul(ps_t[c % 2][:, j * P:(j + 1) * P], hT[:, c * CH + j * P:c * CH + (j + 1) * P],
                                   ident[:, :], start=True, stop=True)
                mm.then_inc(out_prod, 1)

        @block.scalar
        def _(act):
            act.preload_act_table_set("natural_log_exp_and_others")
            act.sem_inc(proj_copied, 2)
            for s in exp_done + log_done:
                act.sem_inc(s, 1)

            def store(rows_of_chunk, c, copies, half):
                def to(table):
                    act.wait_ge(proj_copied, copies + 2)
                    act.dma_start(table_rows[table][bass.ds(c, 1)].rearrange("c p j f -> (c p) j f"),
                                  rows_of_chunk.rearrange("p (j f) -> p j f", f=F)).then_inc(table_in, 16)

                if isinstance(half, int):
                    to(half)
                else:
                    with act.If(half > 0):
                        to(1)
                    with act.Else():
                        to(0)

            def project(table, c, half):
                act.wait_ge(proj_done, table * NCH + c + 1)
                act.copy(stage[:, c, :], ps_t[c % 2]).then_inc(proj_copied, 1)
                store(stage[:, c, :], c, table * NCH + c + 1, half)

            for c in range(NCH):
                project(0, c, 0)
            act.wait_ge(consts_set, 6)
            act.wait_ge(pre, 10)
            act.activation(cut[:, :], cut[:, :], ACT.Sin, bias=half_pi[:, :], scale=-math.pi / CUTOFF
                           ).then_inc(cosine_done, 1)
            act.preload_act_table_set("natural_log_exp_and_others")
            b2_loads(act, 0)
            act.wait_ge(agg_clear, 1)
            act.copy(scratch[:, TABLES:TABLES + NP], aggT[:, :]).then_inc(act_cleared, 1)
            act.copy(scratch[:, TABLES + NP:CLEAR_ACT], aggT[:, :]).then_inc(act_cleared, 1)
            K = load_passes(act)

            def chunk_softplus(done):
                act.wait_ge(n_clamp, done)
                act.activation(step_one, step_one, ACT.Exp).then_inc(n_exp, 1)
                act.wait_ge(n_exp, done)
                act.activation(step_one, step_one, ACT.Ln, bias=half_col[:, :], scale=0.5).then_inc(n_act, 1)

            def chunk_store(c, done, half):
                act.wait_ge(proj_done, done + NCH)
                act.wait_ge(table_in, (done + (NCH - 1)) * 16)
                act.copy(stage_one, ps_t[0]).then_inc(proj_copied, 1)
                store(stage_one, c, done + NCH, half)

            act.wait_ge(early_set, 1)
            with act.Fori(0, L0) as layer:
                next_half = act.snap((layer + 1) & 1)
                with act.Fori(0, K) as k:
                    with act.Fori(0, NIT) as it:
                        uses = Uses(act, layer * (K * NIT) + k * NIT + it)
                        for u in range(U):
                            if u == 1:
                                with act.If(load_early(act, it) > 0):
                                    chunk_softplus(layer * NCH + load_early(act, it, 1))
                            if u == 3:
                                with act.If(load_early(act, it) > 0):
                                    early = load_early(act, it, 1)
                                    chunk_store(act.snap(early - 1), layer * NCH + early, next_half)
                            uses.wait(clamp_done, u)
                            act.activation(xc[:, u % 2, :], xc[:, u % 2, :], ACT.Exp).then_inc(exp_done[u % S], 1)
                            uses.wait(exp_done, u)
                            act.activation(lg[:, u % 2, :], xc[:, u % 2, :], ACT.Ln, bias=half_col[:, :], scale=0.5
                                           ).then_inc(log_done[u % S], 1)
                with act.If(load_early(act, NIT - 1) > 0):
                    for (i, half, clamp, value), exp, signal in zip(half_steps(layer, HALF_CLAMP, n_clamp),
                                                                    (half_step, n_exp), (half_step, n_act)):
                        act.wait_ge(clamp, value)
                        act.activation(step_one[:, half], step_one[:, half], ACT.Exp).then_inc(exp, 1)
                        act.wait_ge(exp, value + (HALF_EXP - HALF_CLAMP if i == 0 else 0))
                        act.activation(step_one[:, half], step_one[:, half], ACT.Ln, bias=half_col[:, :], scale=0.5
                                       ).then_inc(signal, 1)
                    for (i, half, proj, value), signal in zip(half_steps(layer, HALF_PROJ, proj_done, NCH),
                                                              (half_step, proj_copied)):
                        act.wait_ge(proj, value)
                        act.wait_ge(table_in, (layer * NCH + (2 * NCH - 1)) * 16)
                        act.copy(stage_one[:, half], ps_t[i][:, 0:CH // 2]).then_inc(signal, 1)
                    act.wait_ge(half_step, layer * HALF_COPIED + HALF_COPIED)
                    store(stage_one, NCH - 1, layer * NCH + 2 * NCH, next_half)
                with act.Else():
                    for c in range(NCH + 2):
                        if c < NCH:
                            act.wait_ge(n_clamp, layer * NCH + c + 1)
                            act.activation(xc[:, c % 2, :], xc[:, c % 2, :], ACT.Exp).then_inc(n_exp, 1)
                            act.wait_ge(n_exp, layer * NCH + c + 1)
                            act.activation(lg[:, c % 2, :], xc[:, c % 2, :], ACT.Ln, bias=half_col[:, :], scale=0.5
                                           ).then_inc(n_act, 1)
                        if c >= 2:
                            project(layer + 1, c - 2, next_half)
                act.wait_ge(proj_done, layer * NCH + 2 * NCH)
                act.wait_ge(h_kept, layer * NCH + NCH + 1)
                act.dma_start(node_w[:, :], node_w_d[bass.ds(layer + 1, 1)].rearrange("a p t -> (a p) t")
                              ).then_inc(node_w_in, 16)
                with act.If(layer < L0 - 1):
                    b2_loads(act, layer + 1)
            act.wait_ge(table_in, (L0 + 1) * NCH * 16)

            def layer_norm(r):
                for c in range(NCH + 3):
                    if c < NCH:
                        act.wait_ge(ln_dev, r * NCH + c + 1)
                        if c >= 2:
                            act.wait_ge(ln_var, r * NCH + c - 1)
                        act.activation(lg[:, c % 2, :], col(hT, c), ACT.Square).then_inc(ln_sq, 1)
                    if 1 <= c <= NCH:
                        d = c - 1
                        act.wait_ge(ln_var, r * NCH + d + 1)
                        if d >= 2:
                            act.wait_ge(ln_done, r * NCH + d - 1)
                        act.activation(ex[:, d % 2, :], ps_w[d % 2][:, :], ACT.Ln, bias=eps_col[:, :]
                                       ).then_inc(ln_log, 1)
                        act.wait_ge(ln_log, r * NCH + d + 1)
                        act.activation(ex[:, d % 2, :], ex[:, d % 2, :], ACT.Exp, scale=-0.5).then_inc(ln_inv, 1)
                    if c >= 3 and r == 0:
                        act.wait_ge(ln_done, c - 2)
                        act.copy(col(xT, c - 3), col(hT, c - 3)).then_inc(ln_keep, 1)

            layer_norm(0)
            def gin_relu(g, c):
                act.wait_ge(n_prod1, (g + L0) * NCH + c + 1)
                if c >= 2:
                    act.wait_ge(n_prod2, (g + L0) * NCH + c - 1)
                act.activation(hid[:, c % 2, :], ps_h[c % 2][:, :], ACT.Relu,
                               bias=gin_w[:, GW_B1:GW_B1 + 1]).then_inc(n_act, 1)

            def keep_turned(g, c):
                act.wait_ge(turned, g * NCH + c + 1)
                if not isinstance(g, int):
                    act.wait_ge(lo_done, g * NCH + c + 1 - NCH)
                act.copy(stage[:, c, :], ps_a[c % 2][:, :]).then_inc(staged, 1)

            act.sem_inc(agg_in, 2)
            act.sem_inc(agg_sum, 1)
            most = load_most_edges(act)
            with act.If(most > COUNT_MAX):
                with act.Fori(0, L1) as g:
                    for c in range(NCH):
                        project(g + (L0 + 1), c, 0)
                    act.sem_inc(agg_in, NCH)
                    act.wait_ge(gin_w_in, g * 16 + 16)
                    for c in range(NCH):
                        gin_relu(g, c)
            with act.Else():
                for c in range(NCH - 1):
                    keep_turned(0, c)
                with act.Fori(0, L1) as g:
                    for c in range(NCH + 1):
                        if c == NCH - 1:
                            act.wait_ge(turned, g * NCH + NCH)
                            act.copy(stage[:, c, :], ps_a[c % 2][:, :]).then_inc(staged, 1)
                        if c < NCH:
                            act.wait_ge(agg_sum, g * NCH + 1)
                            act.wait_ge(staged, g * NCH + c + 1)
                            act.copy(col(hi, c), stage[:, c, :]).then_inc(hi_done, 1)
                        if c >= 1:
                            act.wait_ge(rest_done, g * NCH + c)
                            act.copy(col(mid, c - 1), stage[:, c - 1, :]).then_inc(mid_done, 1)
                    for c in range(NCH + 1):
                        if c == 1:
                            act.wait_ge(gin_w_in, g * 16 + 16)
                        if c >= 1:
                            gin_relu(g, c - 1)
                        if c < NCH:
                            if c >= 2:
                                keep_turned(g + 1, c - 2)
                            act.wait_ge(agg_sum, g * NCH + c + 2)
                            act.copy(aggT[:, c * CH:c * CH + nodes_in(c)], ps_t[c % 2][:, 0:nodes_in(c)]
                                     ).then_inc(agg_in, 1)
                    keep_turned(g + 1, NCH - 2)
            layer_norm(1)
            for c in range(NCH):
                act.wait_ge(out_prod, c + 1)
                act.copy(stage[:, c, :], ps_t[c % 2]).then_inc(out_copied, 1)
                act.wait_ge(out_copied, c + 1)
                full = min((N - c * CH) // P, CH // P)
                act.dma_start(out_d[c * CH:c * CH + full * P, :].rearrange("(j p) f -> p j f", p=P),
                              stage[:, c, 0:full * F].rearrange("p (j f) -> p j f", f=F)).then_inc(out_done, 16)
                rest = min(N - c * CH, CH) - full * P
                if rest:
                    act.dma_start(out_d[c * CH + full * P:N, :], stage[0:rest, c, full * F:(full + 1) * F]
                                  ).then_inc(out_done, 16)
            act.wait_ge(out_done, 16 * (NCH + (1 if N % P else 0)))

        @block.vector
        def _(dve):
            for s in clamp_done + ssp_done + msg_done + equal_done + hot_done + add_done + tile_hot + [count_added]:
                dve.sem_inc(s, 1)
            dve.sem_inc(gin_w_free, 1)
            dve.sem_inc(h_kept, 1)
            dve.memset(aggT[:, :], 0.0).then_inc(agg_clear, 1)
            dve.wait_ge(dst_in, 16)
            dst_f = rel
            dve.tensor_copy(dst_f[:, :], dst_i).then_inc(pre, 1)
            dve.wait_ge(pre, 1)
            grouped = dst_f[:, :].rearrange("p (g t) -> p g t", t=TPG)
            dve.tensor_reduce(base_f[:, :], grouped, AX.X, ALU.min)
            dve.tensor_reduce(ends[:, 1, :], grouped, AX.X, ALU.max).then_inc(pre, 1)
            dve.wait_ge(pre, 2)
            dve.tensor_scalar(ends[:, 0, :], base_f[:, :], -1.0, None, ALU.mult).then_inc(pre, 1)

            def prepare_edge_weights(layer):
                dve.wait_ge(edge_w_in, layer * 32 + 32)
                dve.tensor_scalar(b1_ln2[:, :], edge_w[:, EW_B1:EW_B1 + 1], -LN2, None, ALU.add).then_inc(b1_set, 1)
                for r in range(3):
                    rest = b2_row[:, :] if r == 0 else b2_rest[:, r - 1, :]
                    dve.tensor_copy(b2_flat[:, r, :], rest).then_inc(b2_split, 1)
                    if r < 2:
                        dve.wait_ge(b2_split, layer * 5 + 2 * r + 1)
                        dve.tensor_tensor(b2_rest[:, r, :], rest, b2_flat[:, r, :], ALU.subtract).then_inc(b2_split, 1)
                        dve.wait_ge(b2_split, layer * 5 + 2 * r + 2)

            dve.memset(scratch[:, CLEAR_ACT:CLEAR_WAITING], 0.0).then_inc(dve_cleared, 1)
            dve.wait_ge(ends_reduced, 1)
            dve.tensor_scalar(base_f[:, :], ends_all[:, 0, :], -1.0, None, ALU.mult).then_inc(pre, 1)
            dve.tensor_tensor(span, ends_all[:, 0, :], ends_all[:, 1, :], ALU.add).then_inc(pre, 1)
            dve.wait_ge(pre, 5)
            dve.tensor_reduce(span_max[:, :], span, AX.X, ALU.max).then_inc(pre, 1)
            dve.wait_ge(pre, 6)
            dve.tensor_copy(span_i[:, :], span_max[:, :]).then_inc(pre, 1)
            dve.wait_ge(pre, 7)
            dve.tensor_scalar(span_s[:, :], span_i[:, :], WIN.bit_length() - 1, None, ALU.arith_shift_right
                              ).then_inc(pre, 1)
            dve.wait_ge(pre, 8)
            dve.tensor_scalar(passes[:, :], span_s[:, :], 1.0, None, ALU.add).then_inc(pre, 1)
            dve.wait_ge(pre, 9)
            dve.sem_inc(ready, 1)
            dve.wait_ge(consts_in, 16 * 4)
            dve.tensor_scalar(cut[:, :], len_raw, 0.0, CUTOFF, ALU.max, ALU.min).then_inc(pre, 1)
            dve.tensor_scalar(len_mask, len_raw, 0.0, None, ALU.is_ge).then_inc(pre, 1)
            dve.tensor_copy(src_f[:, :], src_i).then_inc(pre, 1)
            dve.wait_ge(plan_in, 16)
            dve.tensor_tensor(plan[:, 0:NG], base_f[:, :], plan[:, 0:NG], ALU.subtract).then_inc(pre, 1)
            dve.tensor_scalar(sorted_dst[:, :], span_max[:, :], float(WIN), None, ALU.is_lt).then_inc(pre, 1)
            dve.wait_ge(pre, 14)
            dve.tensor_reduce(slack[:, :], plan[:, 0:NG], AX.X, ALU.min).then_inc(pre, 1)
            dve.wait_ge(pre, 15)
            dve.scalar_tensor_tensor(out=sorted_dst[:, :], in0=slack[:, :], scalar=0.0, in1=sorted_dst[:, :],
                                     op0=ALU.is_ge, op1=ALU.mult).then_inc(pre, 1)
            dve.wait_ge(pre, 16)
            dve.tensor_scalar(early_now[:, :], plan[:, NG:NG + NIT], sorted_dst[:, :], None, ALU.mult
                              ).then_inc(early_set, 1)
            dve.tensor_tensor(grouped, grouped, base_f[:, :].unsqueeze(2).broadcast_to([P, NG, TPG]),
                              ALU.subtract).then_inc(pre, 1)
            prepare_edge_weights(0)
            dve.memset(scratch[:, CLEAR_WAITING:CLEAR_DVE], 0.0).then_inc(dve_cleared, 1)
            dve.scalar_tensor_tensor(out=len_raw, in0=len_raw, scalar=CUTOFF, in1=len_mask,
                                     op0=ALU.is_le, op1=ALU.mult).then_inc(pre, 1)
            dve.wait_ge(cosine_done, 1)
            dve.tensor_scalar(cut[:, :], cut[:, :], 1.0, 0.5, ALU.add, ALU.mult).then_inc(pre, 1)
            dve.wait_ge(pre, 19)
            dve.tensor_tensor(cut[:, :], cut[:, :], len_raw, ALU.mult).then_inc(pre, 1)
            dve.wait_ge(pre, 20)
            dve.memset(scratch[:, 0:TABLES], 0.0).then_inc(dve_cleared, 1)
            dve.wait_ge(act_cleared, 2)
            dve.wait_ge(pool_cleared, 2)
            dve.wait_ge(dve_cleared, 3)
            K = load_passes(dve)

            def windows_of(t, first, tiles):
                return (win_now[:, :].unsqueeze(1).broadcast_to([P, tiles, WIN]),
                        t[:, first:first + tiles].unsqueeze(2).broadcast_to([P, tiles, WIN]))

            def match(u, signal):
                win, dst = windows_of(rel_now, u * TPG, HB * TPG)
                dve.tensor_tensor(onehot[:, u // HB % 2, :, :], win, dst, ALU.is_equal).then_inc(signal[u % S], 1)

            def weigh(uses, u):
                hot = onehot[:, u // HB % 2, :, :]
                uses.wait(equal_done, u)
                dve.tensor_tensor(hot, hot, windows_of(cut_now, u * TPG, HB * TPG)[1], ALU.mult
                                  ).then_inc(hot_done[u % S], 1)

            def add_window(uses, u, it):
                start = dve.value_load(base_i[0:1, bass.ds(it * U + u, 1)], min_val=0, max_val=START_MAX)
                window = aggT[:, bass.ds(start, WIN)]
                uses.wait(agg_done, u)
                uses.wait(add_done, u - 1)
                dve.tensor_tensor(window, window, ps_a[u % 2][:, 0:WIN], ALU.add).then_inc(add_done[u % S], 1)

            def window_starts(k, turn):
                dve.tensor_copy(win_now[:, :], iota[:, bass.ds(k * WIN, WIN)]).then_inc(win_set, 1)
                dve.wait_ge(win_set, turn * 2 + 1)
                dve.tensor_scalar(base_i[:, :], base_f[:, :], win_now[:, 0:1], float(START_MAX), ALU.add, ALU.min
                                  ).then_inc(win_set, 1)

            def count_slices_now(b, n):
                dve.tensor_copy(rel_count[:, :], rel[:, bass.ds(b * BT, BT)]).then_inc(count_slices, 1)
                dve.tensor_copy(src_count[:, :], src_f[:, bass.ds(b * BT, BT)]).then_inc(count_slices, 1)
                dve.wait_ge(count_slices, n * 2 + 2)

            def count_hot(uses, q):
                before = q - 2
                uses.wait_count(tile_counted[before % TPG], before // TPG)
                if q % TPG == 0:
                    win, dst = windows_of(rel_count, q, TPG)
                    dve.tensor_tensor(dst_hot[:, q // TPG % 2, :, :], win, dst, ALU.is_equal)
                dve.tensor_scalar(src_hot[:, q % 2, :], iota[:, :], src_count[:, q:q + 1], None, ALU.is_equal
                                  ).then_inc(tile_hot[q % TPG], 1)

            def add_counts(uses, j, b):
                start = dve.value_load(base_i[0:1, bass.ds(b * BG + j, 1)], min_val=0, max_val=START_MAX)
                window = counts[:, :, bass.ds(start, WIN)]
                uses.wait_count(tile_counted[TPG - 1], j)
                uses.wait_count(count_added, j - 1)
                dve.tensor_tensor(window, window, ps_c.rearrange("p (b w) -> p b w", w=WIN), ALU.add
                                  ).then_inc(count_added, 1)

            def iteration_slices(it, n):
                dve.tensor_copy(rel_now[:, :], rel[:, bass.ds(it * (U * TPG), U * TPG)]).then_inc(slices_set, 1)
                dve.tensor_copy(cut_now[:, :], cut[:, bass.ds(it * (U * TPG), U * TPG)]).then_inc(slices_set, 1)
                dve.wait_ge(slices_set, n * 2 + 2)

            def chunk_clamp(done):
                dve.wait_ge(n_prod1, done)
                dve.tensor_scalar(step_one, ps_t[0], node_w[:, NW_CB2:NW_CB2 + 1], XCLAMP, ALU.add, ALU.min
                                  ).then_inc(n_clamp, 1)

            def chunk_ssp(done):
                dve.wait_ge(n_act, done)
                dve.scalar_tensor_tensor(out=step_one, in0=ps_t[0], scalar=cb2_ln2[:, :],
                                         in1=step_one, op0=ALU.add, op1=ALU.max).then_inc(n_ssp, 1)

            def chunk_h(start, done):
                dve.wait_ge(n_prod2, done)
                dve.wait_ge(h_kept, done)
                for out, signal in ((step_one, h_done), (hT[:, bass.ds(start, CH)], h_kept)):
                    dve.scalar_tensor_tensor(out=out, in0=ps_t[1], scalar=node_w[:, NW_LB:NW_LB + 1],
                                             in1=hT[:, bass.ds(start, CH)], op0=ALU.add, op1=ALU.add
                                             ).then_inc(signal, 1)

            def after_edges(layer):
                with dve.If(layer < L0 - 1):
                    prepare_edge_weights(layer + 1)
                with dve.Else():
                    dve.tensor_reduce(most_edges[:, :], counts[:, NB, 0:N], AX.X, ALU.max).then_inc(pre, 1)
                    dve.wait_ge(pre, 21)
                    dve.tensor_scalar(most_edges_i[:, :], most_edges[:, :], float(COUNT_MAX + 1), None, ALU.min
                                      ).then_inc(counts_ready, 1)

            with dve.Fori(0, L0) as layer:
                dve.wait_ge(node_w_in, layer * 16 + 16)
                dve.tensor_scalar(cb2_ln2[:, :], node_w[:, NW_CB2:NW_CB2 + 1], -LN2, None, ALU.add
                                  ).then_inc(cb2_set, 1)
                with dve.Fori(0, K) as k:
                    dve.wait_ge(b1_set, layer + 1)
                    dve.wait_ge(cb2_set, layer + 1)
                    dve.wait_ge(agg_clear, layer + 1)
                    window_starts(k, layer * K + k)
                    with dve.Fori(0, NIT) as it:
                        n = dve.snap(layer * (K * NIT) + k * NIT + it)
                        dve.wait_ge(win_set, (layer * K + k) * 2 + 2)
                        uses = Uses(dve, n)
                        iteration_slices(it, n)
                        turn = layer * K + k
                        counted = dve.snap(layer * NIT + it)
                        count_slices_now(counted, n)
                        for i in range(U + 5):
                            if i < U:
                                uses.wait(mm1_done, i)
                                dve.tensor_scalar(xc[:, i % 2, :], ps_h[i % 2][:, :], edge_w[:, EW_B1:EW_B1 + 1],
                                                  XCLAMP, ALU.add, ALU.min).then_inc(clamp_done[i % S], 1)
                            u = i - 1
                            if 0 <= u < U:
                                uses.wait(log_done, u)
                                dve.scalar_tensor_tensor(out=hid[:, u % 3, :], in0=ps_h[u % 2][:, :],
                                                         scalar=b1_ln2[:, :], in1=lg[:, u % 2, :],
                                                         op0=ALU.add, op1=ALU.max).then_inc(ssp_done[u % S], 1)
                            if i >= 5:
                                add_window(uses, i - 5, it)
                            u = i - 3
                            if 0 <= u < U:
                                if u % HB == 0:
                                    match(u, equal_done)
                                uses.wait(mm2_done, u)
                                wait_rows(dve, turn, it, u)
                                dve.tensor_tensor(msg[:, u % 3, :], ps_w[u % 2][:, :], rows[:, u % S, :], ALU.mult
                                                  ).then_inc(msg_done[u % S], 1)
                                if u % HB == 0:
                                    weigh(uses, u)
                            if i == 0:
                                with dve.If(load_early(dve, it) > 0):
                                    chunk_clamp(layer * NCH + load_early(dve, it, 1))
                            if i == 1:
                                with dve.If(load_early(dve, it) > 0):
                                    chunk_ssp(layer * NCH + load_early(dve, it, 1))
                            if i == 2:
                                with dve.If(load_early(dve, it) > 0):
                                    early = load_early(dve, it, 1)
                                    chunk_h(dve.snap(early * CH - CH), layer * NCH + early)
                            if i in COUNT_STEP:
                                count_hot(uses, COUNT_STEP[i])
                            if i - 2 in COUNT_STEP and COUNT_STEP[i - 2] % TPG == TPG - 1:
                                add_counts(uses, COUNT_STEP[i - 2] // TPG, counted)
                with dve.If(load_early(dve, NIT - 1) > 0):
                    for (i, half, prod1, value), signal in zip(half_steps(layer, HALF_PROD1, n_prod1), (half_step, n_clamp)):
                        dve.wait_ge(prod1, value)
                        dve.tensor_scalar(step_one[:, half], ps_h[i][:, 0:CH // 2], node_w[:, NW_CB2:NW_CB2 + 1],
                                          XCLAMP, ALU.add, ALU.min).then_inc(signal, 1)
                    for (i, half, act, value), signal in zip(half_steps(layer, HALF_ACT, n_act), (half_step, n_ssp)):
                        dve.wait_ge(act, value)
                        dve.scalar_tensor_tensor(out=step_one[:, half], in0=ps_h[i][:, 0:CH // 2], scalar=cb2_ln2[:, :],
                                                 in1=step_one[:, half], op0=ALU.add, op1=ALU.max).then_inc(signal, 1)
                    for out, signals in ((step_one, (half_step, h_done)), (col(hT, NCH - 1), (None, h_kept))):
                        for (i, half, prod2, value), signal in zip(half_steps(layer, HALF_PROD2, n_prod2), signals):
                            if out is step_one:
                                dve.wait_ge(prod2, value)
                                dve.wait_ge(h_kept, layer * NCH + NCH)
                            op = dve.scalar_tensor_tensor(out=out[:, half], in0=ps_w[i][:, 0:CH // 2],
                                                          scalar=node_w[:, NW_LB:NW_LB + 1],
                                                          in1=col(hT, NCH - 1)[:, half], op0=ALU.add, op1=ALU.add)
                            if signal is not None:
                                op.then_inc(signal, 1)
                with dve.Else():
                    for c in range(NCH + 2):
                        if c < NCH:
                            dve.wait_ge(n_prod1, layer * NCH + c + 1)
                            dve.tensor_scalar(xc[:, c % 2, :], ps_h[c % 2][:, :], node_w[:, NW_CB2:NW_CB2 + 1],
                                              XCLAMP, ALU.add, ALU.min).then_inc(n_clamp, 1)
                        if 1 <= c <= NCH:
                            d = c - 1
                            dve.wait_ge(n_act, layer * NCH + d + 1)
                            dve.scalar_tensor_tensor(out=hid[:, d % 2, :], in0=ps_h[d % 2][:, :], scalar=cb2_ln2[:, :],
                                                     in1=lg[:, d % 2, :], op0=ALU.add, op1=ALU.max).then_inc(n_ssp, 1)
                        if c >= 2:
                            d = c - 2
                            dve.wait_ge(n_prod2, layer * NCH + d + 1)
                            dve.scalar_tensor_tensor(out=col(hT, d), in0=ps_w[d % 2][:, :],
                                                     scalar=node_w[:, NW_LB:NW_LB + 1], in1=col(hT, d),
                                                     op0=ALU.add, op1=ALU.add).then_inc(h_done, 1)
                    dve.sem_inc(h_kept, NCH)
                after_edges(layer)
                with dve.If(layer < L0 - 1):
                    dve.memset(aggT[:, :], 0.0).then_inc(agg_clear, 1)

            def layer_norm(r):
                for c in range(NCH + 2):
                    if c == 0:
                        dve.tensor_tensor(col(hT, 0), col(hT, 0), col(xT, 0), ALU.add).then_inc(ln_sum, 1)
                    if c + 1 < NCH:
                        dve.tensor_tensor(col(hT, c + 1), col(hT, c + 1), col(xT, c + 1), ALU.add).then_inc(ln_sum, 1)
                    if c < NCH:
                        dve.wait_ge(ln_mean, r * NCH + c + 1)
                        dve.tensor_tensor(col(hT, c), col(hT, c), ps_h[c % 2][:, :], ALU.subtract
                                          ).then_inc(ln_dev, 1)
                    if c >= 2:
                        d = c - 2
                        dve.wait_ge(ln_inv, r * NCH + d + 1)
                        y, v, step = ex[:, d % 2, :], ps_w[d % 2][:, :], xc[:, d % 2, :]
                        for n, (out, in0, scalar, op, other) in enumerate((
                                (step, v, LN_EPS, ALU.add, y),
                                (step, step, -0.5, ALU.mult, y),
                                (step, step, 1.5, ALU.add, y))):
                            if n:
                                dve.wait_ge(ln_newton, (r * NCH + d) * 3 + n)
                            dve.scalar_tensor_tensor(out=out, in0=in0, scalar=scalar, in1=other, op0=op, op1=ALU.mult
                                                     ).then_inc(ln_newton, 1)
                        dve.wait_ge(ln_newton, (r * NCH + d) * 3 + 3)
                        dve.tensor_tensor(col(hT, d), col(hT, d), step, ALU.mult).then_inc(ln_done, 1)

            dve.wait_ge(x_in, 16)
            dve.wait_ge(h_kept, L0 * NCH + 1)
            dve.wait_ge(proj_done, (L0 + 1) * NCH)
            layer_norm(0)
            def set_eps1(g):
                dve.wait_ge(gin_w_in, g * 16 + 16)
                dve.tensor_scalar(eps1[:, :], gin_w[:, GW_EPS:GW_EPS + 1], 1.0, None, ALU.add).then_inc(eps1_set, 1)

            def gin_z(g, c):
                dve.wait_ge(eps1_set, g + 1)
                dve.wait_ge(agg_in, g * NCH + c + 3)
                if c >= 2:
                    dve.wait_ge(n_prod1, (g + L0) * NCH + c - 1)
                dve.scalar_tensor_tensor(out=xc[:, c % 2, :], in0=col(hT, c), scalar=eps1[:, :],
                                         in1=col(aggT, c), op0=ALU.mult, op1=ALU.add).then_inc(z_done, 1)

            def gin_h(g, c):
                dve.wait_ge(n_prod2, (g + L0) * NCH + c + 1)
                dve.tensor_scalar(col(hT, c), ps_w[c % 2][:, :], gin_w[:, GW_B2:GW_B2 + 1], None, ALU.add
                                  ).then_inc(h_done, 1)

            most = load_most_edges(dve)
            with dve.If(most > COUNT_MAX):
                with dve.Fori(0, L1) as g:
                    set_eps1(g)
                    dve.memset(aggT[:, :], 0.0).then_inc(agg_clear, 1)
                    with dve.Fori(0, K) as k:
                        dve.wait_ge(eps1_set, g + 1)
                        dve.wait_ge(agg_clear, g + (L0 + 1))
                        window_starts(k, (g + L0) * K + k)
                        with dve.Fori(0, NIT) as it:
                            n = dve.snap((g + L0) * (K * NIT) + k * NIT + it)
                            dve.wait_ge(win_set, ((g + L0) * K + k) * 2 + 2)
                            uses = Uses(dve, n)
                            iteration_slices(it, n)
                            for i in range(U + 1):
                                if i < U and i % HB == 0:
                                    match(i, hot_done)
                                if i >= 1:
                                    add_window(uses, i - 1, it)
                                    dve.sem_inc(msg_done[(i - 1) % S], 1)
                    for c in range(NCH + 2):
                        if c < NCH:
                            gin_z(g, c)
                        if c >= 2:
                            gin_h(g, c - 2)
                    dve.wait_ge(h_done, (g + L0 + 1) * NCH)
                    dve.sem_inc(gin_w_free, 1)
            with dve.Else():
                with dve.Fori(0, L1) as g:
                    for c in range(NCH + 1):
                        if c < NCH:
                            dve.wait_ge(hi_done, g * NCH + c + 1)
                            dve.tensor_tensor(stage[:, c, :], stage[:, c, :], col(hi, c), ALU.subtract
                                              ).then_inc(rest_done, 1)
                        if c >= 1:
                            dve.wait_ge(mid_done, g * NCH + c)
                            dve.tensor_tensor(col(lo, c - 1), stage[:, c - 1, :],
                                              col(mid, c - 1), ALU.subtract).then_inc(lo_done, 1)
                    set_eps1(g)
                    for c in range(NCH):
                        gin_z(g, c)
                        gin_h(g, c)
                    dve.wait_ge(h_done, (g + L0 + 1) * NCH)
                    dve.sem_inc(gin_w_free, 1)
            dve.wait_ge(ln_keep, NCH)
            layer_norm(1)


def kernel(x, src, dst, edge_attr_100, edge_weight, L0_gnn_mlp_w1, L0_gnn_mlp_b1, L0_gnn_mlp_w2, L0_gnn_mlp_b2,
           L0_gnn_conv_w1, L0_gnn_conv_w2, L0_gnn_conv_b2, L0_gnn_lin_w, L0_gnn_lin_b,
           L1_gnn_W1, L1_gnn_b1, L1_gnn_W2, L1_gnn_b2, L1_gnn_eps):
    import numpy as np
    import concourse.bacc as bacc
    from concourse.bass_utils import run_bass_kernel_spmd

    def arr(a):
        return np.asarray(a)

    def padded(a, n, value=0):
        return np.concatenate([a, np.full((n - a.shape[0],) + a.shape[1:], value, a.dtype)])

    def by_column(a):
        return np.ascontiguousarray(a.reshape(NG * TPG, P).T)

    xT = np.ascontiguousarray(padded(arr(x), NP).T)
    src_g = np.ascontiguousarray(padded(arr(src), EP).reshape(NG, TPG, P).transpose(0, 2, 1))
    src_c = by_column(padded(arr(src), EP))
    dst_c = by_column(padded(arr(dst), EP, N))
    ew_c = by_column(padded(arr(edge_weight), EP))
    attr = np.ascontiguousarray(padded(arr(edge_attr_100), EP).reshape(NG, GE, G).transpose(0, 2, 1))
    plan = np.zeros((P, NG + NIT), np.float32)
    for c, it in enumerate(EARLY_AT):
        plan[:, it * U:NG] = (c + 1) * CH
        plan[:, NG + it] = c + 1
    w1 = np.zeros((L0, P, F), np.float32)
    w1[:, :G] = arr(L0_gnn_mlp_w1)
    edge_w = np.concatenate([w1, arr(L0_gnn_mlp_w2), arr(L0_gnn_mlp_b1)[:, :, None]], axis=2)
    first_w = np.ascontiguousarray(arr(L0_gnn_conv_w1)[0])
    next_w = np.roll(arr(L0_gnn_conv_w1), -1, axis=0)
    edge_w = np.concatenate([edge_w, edge_w[:1]])
    b2_row = np.ascontiguousarray(arr(L0_gnn_mlp_b2)[:, None, :])
    b2_row = np.concatenate([b2_row, b2_row[:1]])
    node_w = np.concatenate([arr(L0_gnn_conv_w2), arr(L0_gnn_lin_w), next_w, arr(L0_gnn_conv_b2)[:, :, None],
                             arr(L0_gnn_lin_b)[:, :, None]], axis=2)
    node_w = np.concatenate([node_w, node_w[:1]])
    eps = np.ascontiguousarray(np.broadcast_to(arr(L1_gnn_eps)[:, None, None], (L1, P, 1)))
    gin_w = np.concatenate([arr(L1_gnn_W1), arr(L1_gnn_W2), arr(L1_gnn_b1)[:, :, None],
                            arr(L1_gnn_b2)[:, :, None], eps], axis=2)
    ident = np.eye(P, dtype=np.float32)
    iota = np.ascontiguousarray(np.broadcast_to(np.arange(NP, dtype=np.int16), (P, NP)))

    nc = bacc.Bacc("TRN2", target_bir_lowering=False, num_devices=1)
    arrays, args = {}, []
    for name, a in (("xT", xT), ("src", src_g), ("src_by_column", src_c), ("dst", dst_c), ("plan", plan), ("edge_len", ew_c), ("attr", attr),
                    ("edge_w", edge_w), ("b2_row", b2_row), ("first_w", first_w), ("node_w", node_w), ("gin_w", gin_w),
                    ("ident", ident), ("iota", iota)):
        arrays[f"in_{name}"] = a
        args.append(nc.dram_tensor(f"in_{name}", a.shape, mybir.dt.from_np(a.dtype), kind="ExternalInput").ap())
    out = nc.dram_tensor("out", (N, F), mybir.dt.float32, kind="ExternalOutput").ap()
    gnn_program(nc, *args, out)
    return run_bass_kernel_spmd(nc, [arrays], core_ids=[0]).results[0]["out"]
```
